# Optimizing a Trainium2 kernel written in Bass

```python
import numpy as np
import jax
import jax.numpy as jnp

def _softmax(x, axis=-1):
    return jax.nn.softmax(x, axis=axis)

def _gelu(x):
    return jax.nn.gelu(x, approximate=True)

def _silu(x):
    return jax.nn.silu(x)

def _sigmoid(x):
    return jax.nn.sigmoid(x)

def _layernorm(x, axis=-1, eps=1e-05):
    m = jnp.mean(x, axis=axis, keepdims=True)
    v = jnp.var(x, axis=axis, keepdims=True)
    return (x - m) / jnp.sqrt(v + eps)

def _scatter_add(tgt, idx, src, axis=0):
    return tgt.at[idx].add(src)

def _segment_sum(src, seg, n):
    return jax.ops.segment_sum(src, seg, n)
kernel_name = 'mk_recurrent_d2_jaxref_r8_245361'

def setup_inputs(seed: int=0):
    np.random.seed(seed)
    _w = jnp.asarray

    def _L0_attn_setup():
        import jax, jax.numpy as jnp
        import numpy as np
        D_MODEL = 128
        D_STATE = 128
        MLP_RATIO = 2
        LN_EPS = 1e-05

        def _layernorm(x, g, b):
            mu = jnp.mean(x, axis=-1, keepdims=True)
            var = jnp.var(x, axis=-1, keepdims=True)
            return (x - mu) * jax.lax.rsqrt(var + LN_EPS) * g + b

        def _lru(u, w_in, log_lambda, w_out, D_skip):
            lam = jax.nn.sigmoid(log_lambda)
            u_proj = jnp.einsum('btd,sd->bts', u, w_in)
            B, T, S = u_proj.shape

            def step(x, u_t):
                x = lam * x + (1.0 - lam) * u_t
                return (x, x)
            x0 = jnp.zeros((B, S), dtype=u_proj.dtype)
            _, ys = jax.lax.scan(step, x0, jnp.swapaxes(u_proj, 0, 1))
            y_states = jnp.swapaxes(ys, 0, 1)
            return jnp.einsum('bts,ds->btd', y_states, w_out) + u * D_skip
        key = jax.random.key(seed)
        ks = jax.random.split(key, 8)
        B, T = (4, 512)
        d, s, f = (D_MODEL, D_STATE, D_MODEL * MLP_RATIO)
        inp = {'x': jax.random.normal(ks[0], (B, T, d), dtype=jnp.float32), 'w_in': jax.random.normal(ks[1], (s, d), dtype=jnp.float32) / np.sqrt(d), 'log_lambda': jnp.full((s,), 2.0, dtype=jnp.float32), 'w_out': jax.random.normal(ks[2], (d, s), dtype=jnp.float32) / np.sqrt(s), 'D_skip': jnp.full((d,), 0.1, dtype=jnp.float32), 'ln1_g': jnp.ones((d,), dtype=jnp.float32), 'ln1_b': jnp.zeros((d,), dtype=jnp.float32), 'ln2_g': jnp.ones((d,), dtype=jnp.float32), 'ln2_b': jnp.zeros((d,), dtype=jnp.float32), 'w1': jax.random.normal(ks[3], (f, d), dtype=jnp.float32) / np.sqrt(d), 'b1': jnp.zeros((f,), dtype=jnp.float32), 'w2': jax.random.normal(ks[4], (d, f), dtype=jnp.float32) / np.sqrt(f), 'b2': jnp.zeros((d,), dtype=jnp.float32)}
        return inp
    _L0_attn_in = _L0_attn_setup()

    def _L0_ffn_setup():
        import jax, jax.numpy as jnp
        import numpy as np
        B, S, H, I, E, K = (2, 64, 128, 64, 64, 8)
        key = jax.random.key(seed)
        ks = jax.random.split(key, 8)
        return {'hidden_states': jax.random.normal(ks[0], (B, S, H), dtype=jnp.float32), 'router_w': jax.random.normal(ks[1], (H, E), dtype=jnp.float32) * 0.02, 'shared_gate_w': jax.random.normal(ks[2], (H, I), dtype=jnp.float32) * 0.02, 'shared_up_w': jax.random.normal(ks[3], (H, I), dtype=jnp.float32) * 0.02, 'shared_down_w': jax.random.normal(ks[4], (I, H), dtype=jnp.float32) * 0.02, 'expert_gate_k': jax.random.normal(ks[5], (E, H, I), dtype=jnp.float32) * 0.02, 'expert_up_k': jax.random.normal(ks[6], (E, H, I), dtype=jnp.float32) * 0.02, 'expert_down_k': jax.random.normal(ks[7], (E, I, H), dtype=jnp.float32) * 0.02}
    _L0_ffn_in = _L0_ffn_setup()

    def _L1_attn_setup():
        import jax, jax.numpy as jnp
        import numpy as np
        D_MODEL = 128
        N_HEAD = 16
        SEQ = 256
        BATCH = 2
        key = jax.random.key(seed)
        x = jax.random.normal(key, (BATCH, SEQ, D_MODEL), dtype=jnp.float32)
        return {'x': x}
    _L1_attn_in = _L1_attn_setup()

    def _L1_ffn_setup():
        import jax, jax.numpy as jnp
        import numpy as np
        TOPK = 4
        key = jax.random.key(seed)
        ks = jax.random.split(key, 9)
        B, T, D = (4, 256, 128)
        E, H = (32, 128)
        HS = H * TOPK
        s = lambda k, shape, fan: jax.random.normal(k, shape, dtype=jnp.float32) / np.sqrt(fan)
        return {'x': jax.random.normal(ks[0], (B, T, D), dtype=jnp.float32), 'router_w': s(ks[1], (E, D), D), 'router_bias': jnp.zeros((E,), dtype=jnp.float32), 'gate_w': s(ks[2], (E, H, D), D), 'up_w': s(ks[3], (E, H, D), D), 'down_w': s(ks[4], (E, D, H), H), 'sgate_w': s(ks[5], (HS, D), D), 'sup_w': s(ks[6], (HS, D), D), 'sdown_w': s(ks[7], (D, HS), HS)}
    _L1_ffn_in = _L1_ffn_setup()
    _d = {'L0_attn_x': _L0_attn_in['x'], 'L0_attn_w_in': _L0_attn_in['w_in'], 'L0_attn_log_lambda': _L0_attn_in['log_lambda'], 'L0_attn_w_out': _L0_attn_in['w_out'], 'L0_attn_D_skip': _L0_attn_in['D_skip'], 'L0_attn_ln1_g': _L0_attn_in['ln1_g'], 'L0_attn_ln1_b': _L0_attn_in['ln1_b'], 'L0_attn_ln2_g': _L0_attn_in['ln2_g'], 'L0_attn_ln2_b': _L0_attn_in['ln2_b'], 'L0_attn_w1': _L0_attn_in['w1'], 'L0_attn_b1': _L0_attn_in['b1'], 'L0_attn_w2': _L0_attn_in['w2'], 'L0_attn_b2': _L0_attn_in['b2'], 'L0_ffn_router_w': _L0_ffn_in['router_w'], 'L0_ffn_shared_gate_w': _L0_ffn_in['shared_gate_w'], 'L0_ffn_shared_up_w': _L0_ffn_in['shared_up_w'], 'L0_ffn_shared_down_w': _L0_ffn_in['shared_down_w'], 'L0_ffn_expert_gate_k': _L0_ffn_in['expert_gate_k'], 'L0_ffn_expert_up_k': _L0_ffn_in['expert_up_k'], 'L0_ffn_expert_down_k': _L0_ffn_in['expert_down_k'], 'L1_ffn_router_w': _L1_ffn_in['router_w'], 'L1_ffn_router_bias': _L1_ffn_in['router_bias'], 'L1_ffn_gate_w': _L1_ffn_in['gate_w'], 'L1_ffn_up_w': _L1_ffn_in['up_w'], 'L1_ffn_down_w': _L1_ffn_in['down_w'], 'L1_ffn_sgate_w': _L1_ffn_in['sgate_w'], 'L1_ffn_sup_w': _L1_ffn_in['sup_w'], 'L1_ffn_sdown_w': _L1_ffn_in['sdown_w']}
    _x0 = _d['L0_attn_x']
    _d['L0_attn_x'] = jax.random.normal(jax.random.fold_in(jax.random.key(seed), 1), (4, 1024, 128), dtype=_x0.dtype)
    del _x0
    return _d

def reference(L0_attn_x, L0_attn_w_in, L0_attn_log_lambda, L0_attn_w_out, L0_attn_D_skip, L0_attn_ln1_g, L0_attn_ln1_b, L0_attn_ln2_g, L0_attn_ln2_b, L0_attn_w1, L0_attn_b1, L0_attn_w2, L0_attn_b2, L0_ffn_router_w, L0_ffn_shared_gate_w, L0_ffn_shared_up_w, L0_ffn_shared_down_w, L0_ffn_expert_gate_k, L0_ffn_expert_up_k, L0_ffn_expert_down_k, L1_ffn_router_w, L1_ffn_router_bias, L1_ffn_gate_w, L1_ffn_up_w, L1_ffn_down_w, L1_ffn_sgate_w, L1_ffn_sup_w, L1_ffn_sdown_w):

    def _L0_attn_ref(x, w_in, log_lambda, w_out, D_skip, ln1_g, ln1_b, ln2_g, ln2_b, w1, b1, w2, b2):
        import jax, jax.numpy as jnp
        import numpy as np
        D_MODEL = 128
        D_STATE = 128
        MLP_RATIO = 2
        LN_EPS = 1e-05

        def _layernorm(x, g, b):
            mu = jnp.mean(x, axis=-1, keepdims=True)
            var = jnp.var(x, axis=-1, keepdims=True)
            return (x - mu) * jax.lax.rsqrt(var + LN_EPS) * g + b

        def _lru(u, w_in, log_lambda, w_out, D_skip):
            lam = jax.nn.sigmoid(log_lambda)
            u_proj = jnp.einsum('btd,sd->bts', u, w_in)
            B, T, S = u_proj.shape

            def step(x, u_t):
                x = lam * x + (1.0 - lam) * u_t
                return (x, x)
            x0 = jnp.zeros((B, S), dtype=u_proj.dtype)
            _, ys = jax.lax.scan(step, x0, jnp.swapaxes(u_proj, 0, 1))
            y_states = jnp.swapaxes(ys, 0, 1)
            return jnp.einsum('bts,ds->btd', y_states, w_out) + u * D_skip
        x = x + _lru(_layernorm(x, ln1_g, ln1_b), w_in, log_lambda, w_out, D_skip)
        h = _layernorm(x, ln2_g, ln2_b)
        h = jax.nn.relu(jnp.einsum('btd,fd->btf', h, w1) + b1)
        x = x + jnp.einsum('btf,df->btd', h, w2) + b2
        return x

    def _L0_ffn_ref(hidden_states, router_w, shared_gate_w, shared_up_w, shared_down_w, expert_gate_k, expert_up_k, expert_down_k):
        import jax, jax.numpy as jnp
        import numpy as np
        B, S, H, I, E, K = (2, 64, 128, 64, 64, 8)
        logits = jnp.einsum('bsh,he->bse', hidden_states.astype(jnp.float32), router_w)
        affinity = jax.nn.sigmoid(logits)
        top_scores, top_idx = jax.lax.top_k(affinity, K)
        top_w = top_scores / (jnp.sum(top_scores, axis=-1, keepdims=True) + 1e-09)
        one_hot = jax.nn.one_hot(top_idx, E, dtype=top_w.dtype)
        router_mask = jnp.einsum('bske,bsk->bse', one_hot, top_w).astype(hidden_states.dtype)
        shared = jnp.einsum('bsi,ih->bsh', jax.nn.silu(hidden_states @ shared_gate_w) * (hidden_states @ shared_up_w), shared_down_w)
        gate_out = jnp.einsum('bsh,ehi->bsei', hidden_states, expert_gate_k)
        up_out = jnp.einsum('bsh,ehi->bsei', hidden_states, expert_up_k)
        expert_act = jax.nn.silu(gate_out) * up_out
        routed = jnp.einsum('bsei,eih->bsh', expert_act * router_mask[..., None], expert_down_k)
        return shared + routed

    def _L1_attn_ref(x):
        import jax, jax.numpy as jnp
        import numpy as np
        D_MODEL = 128
        N_HEAD = 16
        SEQ = 256
        BATCH = 2
        B, S, D = x.shape
        H = N_HEAD
        hd = D // H
        qkv = x.reshape(B, S, H, hd).transpose(0, 2, 1, 3)
        q = k = v = qkv
        w = jnp.einsum('bhqd,bhkd->bhqk', q, k) / jnp.sqrt(jnp.asarray(hd, x.dtype))
        causal = jnp.tril(jnp.ones((S, S), dtype=bool))
        mask_value = jnp.finfo(w.dtype).min
        w = jnp.where(causal[None, None, :, :], w, mask_value)
        w = jax.nn.softmax(w, axis=-1)
        out = jnp.einsum('bhqk,bhkd->bhqd', w, v)
        return out.transpose(0, 2, 1, 3).reshape(B, S, D)

    def _L1_ffn_ref(x, router_w, router_bias, gate_w, up_w, down_w, sgate_w, sup_w, sdown_w):
        import jax, jax.numpy as jnp
        import numpy as np
        TOPK = 4
        B, T, D = x.shape
        flat = x.reshape(B * T, D)
        logits = flat.astype(jnp.float32) @ router_w.T + router_bias
        scores = jax.nn.softmax(logits, axis=-1)
        topk_scores, topk_idx = jax.lax.top_k(scores, TOPK)
        topk_scores = topk_scores / jnp.clip(topk_scores.sum(axis=-1, keepdims=True), 1e-12, None)
        h = jax.nn.silu(jnp.einsum('nd,ehd->neh', flat, gate_w)) * jnp.einsum('nd,ehd->neh', flat, up_w)
        expert_out = jnp.einsum('neh,edh->ned', h, down_w)
        sel = jnp.take_along_axis(expert_out, topk_idx[:, :, None], axis=1)
        out = (sel * topk_scores.astype(flat.dtype)[:, :, None]).sum(axis=1)
        out = out + jax.nn.silu(flat @ sgate_w.T) * (flat @ sup_w.T) @ sdown_w.T
        return out.reshape(B, T, D)
    x = L0_attn_x
    xn = _layernorm(x, axis=-1)
    s = _L0_attn_ref(xn, L0_attn_w_in, L0_attn_log_lambda, L0_attn_w_out, L0_attn_D_skip, L0_attn_ln1_g, L0_attn_ln1_b, L0_attn_ln2_g, L0_attn_ln2_b, L0_attn_w1, L0_attn_b1, L0_attn_w2, L0_attn_b2)
    g = _silu(_L0_ffn_ref(xn, L0_ffn_router_w, L0_ffn_shared_gate_w, L0_ffn_shared_up_w, L0_ffn_shared_down_w, L0_ffn_expert_gate_k, L0_ffn_expert_up_k, L0_ffn_expert_down_k))
    x = x + s * g
    xn = _layernorm(x, axis=-1)
    s = _L1_attn_ref(xn)
    g = _silu(_L1_ffn_ref(xn, L1_ffn_router_w, L1_ffn_router_bias, L1_ffn_gate_w, L1_ffn_up_w, L1_ffn_down_w, L1_ffn_sgate_w, L1_ffn_sup_w, L1_ffn_sdown_w))
    x = x + s * g
    return x

_drawn_inputs = setup_inputs


def setup_inputs(seed=0):
    import zlib

    import numpy as np

    out = dict(_drawn_inputs(seed))
    spreads = {'L0_attn_log_lambda': (2.0, 0.6),
     'L0_attn_D_skip': (0.10000000149011612, 0.6),
     'L0_attn_ln1_g': (1.0, 0.6),
     'L0_attn_ln1_b': (0.0, 0.8),
     'L0_attn_ln2_g': (1.0, 0.6),
     'L0_attn_ln2_b': (0.0, 0.8),
     'L0_attn_b1': (0.0, 0.8),
     'L0_attn_b2': (0.0, 2.0),
     'L1_ffn_router_bias': (0.0, 2.0)}
    factors = {'L0_attn_w_in': 8.0,
     'L0_attn_w_out': 8.0,
     'L0_attn_w1': 8.0,
     'L0_attn_w2': 8.0,
     'L0_ffn_router_w': 8.0,
     'L0_ffn_shared_gate_w': 8.0,
     'L0_ffn_shared_up_w': 8.0,
     'L0_ffn_shared_down_w': 8.0,
     'L0_ffn_expert_gate_k': 8.0,
     'L0_ffn_expert_up_k': 8.0,
     'L0_ffn_expert_down_k': 8.0,
     'L1_ffn_router_w': 8.0,
     'L1_ffn_gate_w': 8.0,
     'L1_ffn_up_w': 8.0,
     'L1_ffn_down_w': 8.0,
     'L1_ffn_sgate_w': 8.0,
     'L1_ffn_sup_w': 8.0,
     'L1_ffn_sdown_w': 8.0}
    for name, (base, spread) in spreads.items():
        noise = np.random.default_rng([zlib.crc32(name.encode()), seed]).standard_normal(out[name].shape)
        drawn = base * np.exp(spread * noise) if base else spread * noise
        out[name] = jnp.asarray(drawn.astype(out[name].dtype))
    for name, factor in factors.items():
        out[name] = (out[name] * factor).astype(out[name].dtype)
    return out
```

```python
import concourse.bass as bass
from concourse import mybir
from contextlib import ExitStack

P = 128
SEQS, T, D = 4, 1024, 128
CH = 512
NT = CH // P
HALVES = T // CH
CHUNKS = SEQS * HALVES
TILES = SEQS * T // P
E0, I0 = 64, 64
E1 = 32
M0 = E0 * I0 // P
M1 = E1
U0 = M0 + 1
U1 = M1 + 4
HEADS, HD = 16, 8
HG = HEADS // 4
VW = HD + 1
LN_EPS = 1e-5
RING = 4

C_ID, C_OH0, C_OH1, C_SEL = 0, 128, 192, 224
C_END = 224 + 4 * P
V_LL, V_D, V_G1, V_B1, V_G2, V_B2, V_FB, V_B = 0, 1, 2, 3, 4, 5, 6, 8
V_END = 9
S_IN, S_OUT, S_W1, S_W2, S_R0, S_R1 = 0, 128, 256, 512, 768, 832
S_END = 864

M_BANK, Y_BANK = 4, 5
A_BANK, B_BANK, O_BANK = 6, 7, 7

LN_STEPS = 13
PRE0_STEPS = 3 * LN_STEPS + 11
PRE1_STEPS = LN_STEPS + 14
V0_STEPS = HALVES * (PRE0_STEPS + 1) + 1
V1_STEPS = HALVES * (PRE1_STEPS + 1 + HG)

STEPS = [[(g, k) for g in range(HG) for k in range(NT * (half + 1))] for half in range(HALVES)]
STEP0 = [0, len(STEPS[0])]
ALL_STEPS = len(STEPS[0]) + len(STEPS[1])
TAIL = 3


def order1(half):
    entries, s, total = [], 0, len(STEPS[half]) + TAIL
    for t in range(U1):
        if t < HG:
            entries.append(("stack", t))
        entries.append(("unit", t))
        while s < total and s * (U1 - 3) < (t - 1) * total:
            entries.append(("step", s))
            s += 1
    while s < total:
        entries.append(("step", s))
        s += 1
    return entries


ORDER1 = [order1(half) for half in range(HALVES)]
ORDER0 = [("unit", t) for t in range(U0)]


class Beside:

    def __init__(self, parts=iter(())):
        self.parts = parts
        self.due = next(parts, None)

    def after(self, unit):
        while self.due is not None and self.due <= unit:
            self.due = next(self.parts, None)


def two_layers(nc, x, weights0, weights1, small, vectors, bias1, constants, x1, out):
    F, R, I = mybir.dt.float32, mybir.dt.float32r, mybir.dt.int32
    ALU, ACT, AX = mybir.AluOpType, mybir.ActivationFunctionType, mybir.AxisListType
    ctx = ExitStack()
    with ctx:
        def sb(name, shape, dt=F):
            return ctx.enter_context(nc.sbuf_tensor(name, shape, dt))

        def sem(name):
            return ctx.enter_context(nc.semaphore(name))

        x_ln = sb("x_ln", [P, NT, D])
        x_res = sb("x_res", [P, NT, D])
        w_hi = sb("w_hi", [P, U1, 3, P], R)
        w_lo = sb("w_lo", [P, U1, 3, P], R)
        stage = sb("stage", [P, RING, 3 * P])
        x_hi = sb("x_hi", [P, 2, CH], R)
        x_lo = sb("x_lo", [P, 2, CH], R)
        h_hi = sb("h_hi", [P, 2, CH], R)
        h_lo = sb("h_lo", [P, 2, CH], R)
        mask_t = sb("mask_t", [P, 2, CH], R)
        router_hi = sb("router_hi", [P, E0 + E1], R)
        router_lo = sb("router_lo", [P, E0 + E1], R)
        onehot1 = sb("onehot1", [2 * E1, E1], R)
        sel = sb("sel", [P, 4, P], R)
        sel0_keys = sb("sel0_keys", [P, E0 * I0], R)
        sel0 = sel0_keys
        k_stack = sel0_keys[:, :].rearrange("p (g t) -> p g t", g=HG)
        q_stack = sb("q_stack", [P, HG, CH], R)
        gate = sb("gate", [P, 2, CH])
        hid = sb("hid", [P, 2, CH])
        work = sb("work", [P, 8 * CH])
        relu = work[:, 0:2 * CH].rearrange("p (a t) -> p a t", a=2)
        u_t, v_t, y_t, z_t, x2_flat = (work[:, i * CH:(i + 1) * CH] for i in range(2, 7))
        x2 = x2_flat.rearrange("p (t d) -> p t d", t=NT)
        prob = work[:, :].rearrange("p (a j t) -> p a j t", a=2, j=4)
        values = sb("values", [P, HALVES * NT, HEADS, VW])
        xn = sb("xn", [P, NT, D])
        rows = sb("rows", [P, NT, D])
        g_t = sb("g_t", [P, CH])
        heads_out = sel_raw = g_t
        s_rows = sb("s_rows", [P, 2, NT, D])
        msk = sb("msk", [P, NT, P])
        small_sb = sb("small_sb", [P, S_END])
        vec = sb("vec", [P, V_END])
        cst = sb("cst", [P, C_SEL])
        bias_sb = sb("bias_sb", [P, E1])
        lam = sb("lam", [P, 3])
        carry = sb("carry", [P, 1])
        stats = sb("stats", [P, NT, 6])
        mv = sb("mv", [P, NT, 2])
        var = sb("var", [P, NT])
        rstd = sb("rstd", [P, 2, NT])
        newton = sb("newton", [P, NT])
        shift = sb("shift", [P, NT])
        aff = sb("aff", [P, NT, E0])
        scores1 = sb("scores1", [P, NT, E1 + 4])
        picked = sb("picked", [P, NT, E0])
        top8 = sb("top8", [P, NT, 8])
        rsum = sb("rsum", [P, 2, NT])
        rden = sb("rden", [P, NT, 4])
        ident = cst[:, C_ID:C_ID + P]

        ps = ctx.enter_context(nc.psum_tensor("ps", [P, 8, 512], F))

        s_small, s_xln, s_xres = sem("s_small"), sem("s_xln"), sem("s_xres")
        s_stage = [sem(f"s_stage{i}") for i in range(RING)]
        s_store = [sem("s_store0"), sem("s_store1")]
        whi_done = [sem("whi_done0"), sem("whi_done1")]
        wlo_done = [sem("wlo_done0"), sem("wlo_done1")]
        setup_act, setup_dve = sem("setup_act"), sem("setup_dve")
        v_step = sem("v_step")
        waited_dve, waited_pool, waited_sp = map(sem, ("waited_dve", "waited_pool", "waited_sp"))
        names = ("norm_done xn_done pe_xt xhi_done xlo_done pe_logits pe_mask mask_rows mask_done "
                 "y_done pe_gt x_new").split()
        L = [{n: sem(f"{n}{i}") for n in names} for i in range(2)]
        unit = "pe_g pe_u pe_m gate_act gate_done prod_done hid_done hhi_done hlo_done pe_down".split()
        N = [{n: sem(f"{n}{i}") for n in unit} for i in range(2)]
        u0_done, pe_ut, u_done, pe_up, v_done, y_scan = map(sem, "u0_done pe_ut u_done pe_up v_done y_scan".split())
        pe_z, z_done, pe_zt, h0_done, pe_ht, h_done = map(sem, "pe_z z_done pe_zt h0_done pe_ht h_done".split())
        pe_f, relu_done, pe_z2, z2_done, pe_z2t, s_done = map(sem, "pe_f relu_done pe_z2 z2_done pe_z2t s_done".split())
        aff_exp = sem("aff_exp")
        logit_done, score_exp, val_done, y_tanh = map(sem, "logit_done score_exp val_done y_tanh".split())
        pe_stack, q_done, k_done = sem("pe_stack"), sem("q_done"), sem("k_done")
        pe_s, exp_done, causal_done = sem("pe_s"), sem("exp_done"), sem("causal_done")
        pe_pv, o_done, pe_ot, so_done = sem("pe_pv"), sem("o_done"), sem("pe_ot"), sem("so_done")

        def nth(b, half, per_chunk, k):
            return b * (HALVES * per_chunk) + (half * per_chunk + k)

        def first_col(half, k):
            return max(k - NT * half, 0) * P

        def diagonal(half, k):
            return k >= NT * half

        def causal_after(half, s):
            before = 2 * sum(diagonal(0, k) for _, k in STEPS[0]) * half
            return before + 2 * sum(diagonal(half, k) for _, k in STEPS[half][:s + 1])

        ALL_CAUSAL = causal_after(1, len(STEPS[1]) - 1)

        def last_of_group(half, s):
            return 0 <= s < len(STEPS[half]) and STEPS[half][s][1] == NT * (half + 1) - 1

        UNITS, MASKED, ORDER = (U0, U1), (M0, M1), ((ORDER0, ORDER0), ORDER1)

        def slot(layer, half, t):
            return (half * UNITS[layer] + t) % 2

        STAGE_USES = [(U0 + RING - 1 - r) // RING for r in range(RING)]

        def staged(layer, t):
            r = (t + layer * U0) % RING
            return r, 16 * (t // RING + 1) if not layer else 16 * ((t + U0) // RING + 1)

        block = ctx.enter_context(nc.Block())

        @block.sync
        def _(sp):
            def tiles(dram, b, half):
                return dram.rearrange("(t p) d -> p t d", p=P)[:, bass.ds(b * (2 * NT) + half * NT, NT), :]

            def load_ln(src, layer, b, half):
                sp.dma_start(x_ln[:, :, :], tiles(src, b, half)).then_inc(s_xln, 16)

            def load_units(layer, src):
                for t in range(UNITS[layer]):
                    if t >= RING:
                        sp.wait_ge(wlo_done[layer], t - RING + 1)
                    elif layer:
                        sp.wait_ge(wlo_done[0], U0 - RING + t + 1)
                    r, _ = staged(layer, t)
                    sp.dma_start(stage[:, r, :], src[t, :, :]).then_inc(s_stage[r], 16)

            def wait_alone(semaphore, count):
                sp.wait_ge(semaphore, count)
                sp.sem_inc(waited_sp, 1)

            def sequence(layer, b, src, dst, load_next, units=None):
                c = L[layer]
                wait_alone(c["xn_done"], nth(b, 0, 1, 1))
                load_ln(src, layer, b, 1)
                sp.dma_start(x_res[:, :, :], tiles(src, b, 0)).then_inc(s_xres, 16)
                if load_next is not None:
                    wait_alone(c["xn_done"], nth(b, 1, 1, 1))
                    load_next()
                for half in range(HALVES):
                    if half:
                        sp.dma_start(x_res[:, :, :], tiles(src, b, half)).then_inc(s_xres, 16)
                        if units is not None:
                            units()
                    wait_alone(c["x_new"], nth(b, half, 1, 1))
                    sp.dma_start(tiles(dst, b, half), x_res[:, :, :]).then_inc(s_store[layer], 16)
                    wait_alone(s_store[layer], 16 * nth(b, half, 1, 1))

            sp.dma_start(cst[:, :], constants[:, 0:C_SEL]).then_inc(s_small, 16)
            load_ln(x, 0, 0, 0)
            sp.dma_start(vec[:, :], vectors).then_inc(s_small, 16)
            sp.dma_start(sel_raw[:, :], constants[:, C_SEL:C_END]).then_inc(s_small, 16)
            sp.dma_start(small_sb[:, :], small).then_inc(s_small, 16)
            sp.dma_start(bias_sb[:, :], bias1.partition_broadcast(P)).then_inc(s_small, 16)
            load_units(0, weights0)
            with sp.Fori(0, SEQS - 1) as b:
                sequence(0, b, x, x1, lambda: load_ln(x, 0, b + 1, 0))
            sequence(0, SEQS - 1, x, x1, lambda: load_ln(x1, 1, 0, 0), lambda: load_units(1, weights1))
            with sp.Fori(0, SEQS - 1) as b:
                sequence(1, b, x1, out, lambda: load_ln(x1, 1, b + 1, 0))
            sequence(1, SEQS - 1, x1, out, None)

        @block.scalar
        def _(act):
            act.wait_ge(s_small, 80)
            nc.scalar.activation(lam[:, 0:1], vec[:, V_LL:V_LL + 1], ACT.Exp, scale=-1.0).then_inc(setup_act, 1)
            nc.scalar.activation(sel[:, :, :].rearrange("p a b -> p (a b)"), sel_raw[:, :], ACT.Copy).then_inc(setup_act, 1)
            nc.scalar.activation(onehot1[:, :], cst[0:2 * E1, C_OH1:C_OH1 + E1], ACT.Copy).then_inc(setup_act, 1)

            def split_hi(layer, t):
                r, count = staged(layer, t)
                act.wait_ge(s_stage[r], count)
                if layer and t < U0:
                    act.wait_ge(N[0]["pe_down"], nth(SEQS - 1, 1, U0, t + 1))
                nc.scalar.activation(w_hi[:, t, :, :].rearrange("p a b -> p (a b)"), stage[:, r, :],
                                     ACT.Copy).then_inc(whi_done[layer], 1)

            def normalise(src, dst, done):
                for t in range(NT):
                    last = nc.scalar.activation(dst[:, t, :], src[:, t, :], ACT.Identity, bias=shift[:, t:t + 1],
                                                scale=rstd[:, 1, t:t + 1])
                last.then_inc(done, 1)

            def prelude0(b, half):
                c = L[0]

                def at(k, per=1):
                    return nth(b, half, per, k)

                yield 3
                act.wait_ge(c["norm_done"], at(1, 3))
                normalise(x_ln, xn, c["xn_done"])
                yield 6
                act.wait_ge(c["pe_xt"], at(1))
                nc.scalar.activation(x_hi[:, half, :], ps[:, A_BANK, :], ACT.Copy).then_inc(c["xhi_done"], 1)
                yield 8
                act.wait_ge(c["norm_done"], at(2, 3))
                normalise(xn, rows, u0_done)
                yield 9
                act.wait_ge(c["pe_logits"], at(1))
                nc.scalar.activation(aff[:, :, :].rearrange("p t e -> p (t e)"), ps[:, A_BANK, 0:NT * E0], ACT.Exp,
                                     scale=-1.0).then_inc(aff_exp, 1)
                yield 10
                act.wait_ge(pe_ut, at(1))
                nc.scalar.activation(u_t, ps[:, B_BANK, :], ACT.Identity, bias=vec[:, V_B1:V_B1 + 1],
                                     scale=vec[:, V_G1:V_G1 + 1]).then_inc(u_done, 1)
                yield 12
                act.wait_ge(pe_up, at(1))
                nc.scalar.activation(v_t, ps[:, A_BANK, :], ACT.Copy, scale=lam[:, 2:3]).then_inc(v_done, 1)
                yield 20
                act.wait_ge(c["norm_done"], at(3, 3))
                normalise(x2, rows, h0_done)
                yield 22
                act.wait_ge(pe_ht, at(1))
                nc.scalar.activation(v_t, ps[:, B_BANK, :], ACT.Identity, bias=vec[:, V_B2:V_B2 + 1],
                                     scale=vec[:, V_G2:V_G2 + 1]).then_inc(h_done, 1)
                yield 23
                act.wait_ge(c["pe_mask"], at(1))
                nc.scalar.activation(mask_t[:, half, :], ps[:, A_BANK, :], ACT.Copy).then_inc(c["mask_done"], 1)
                yield 25
                for i, bank in enumerate((A_BANK, B_BANK)):
                    act.wait_ge(pe_f, at(i + 1, 2))
                    nc.scalar.activation(relu[:, i, :], ps[:, bank, :], ACT.Relu,
                                         bias=vec[:, V_FB + i:V_FB + i + 1]).then_inc(relu_done, 1)
                yield 27
                act.wait_ge(pe_z2, at(1))
                nc.scalar.activation(z_t, ps[:, A_BANK, :], ACT.Identity, bias=vec[:, V_B:V_B + 1]).then_inc(z2_done, 1)

            def prelude1(b, half):
                c = L[1]

                def at(k, per=1):
                    return nth(b, half, per, k)

                yield 6
                act.wait_ge(c["norm_done"], at(1))
                normalise(x_ln, xn, c["xn_done"])
                yield 8
                act.wait_ge(c["pe_xt"], at(1))
                nc.scalar.activation(x_hi[:, half, :], ps[:, A_BANK, :], ACT.Copy).then_inc(c["xhi_done"], 1)
                yield 15
                act.wait_ge(logit_done, at(1))
                nc.scalar.activation(aff[:, :, 0:E1], aff[:, :, 0:E1], ACT.Exp).then_inc(score_exp, 1)
                yield 22
                act.wait_ge(c["pe_mask"], at(1))
                nc.scalar.activation(mask_t[0:2 * E1, half, :], ps[0:2 * E1, A_BANK, :], ACT.Copy).then_inc(c["mask_done"], 1)

            def chunk(layer, b, half, beside, next_weights=False):
                n, c, units = N[layer], L[layer], UNITS[layer]

                def hi(half, t):
                    a = slot(layer, half, t)
                    act.wait_ge(n["hid_done"], nth(b, half, units, t + 1))
                    if half or t >= 2:
                        act.wait_ge(n["pe_down"], nth(b, half, units, t - 1))
                    nc.scalar.activation(h_hi[:, a, :], hid[:, a, :], ACT.Copy).then_inc(n["hhi_done"], 1)

                def experts_out(half):
                    act.wait_ge(n["pe_down"], nth(b, half, units, units))
                    if layer == 0:
                        nc.scalar.activation(g_t[:, :], ps[:, Y_BANK, :], ACT.Silu).then_inc(c["y_done"], 1)
                    else:
                        nc.scalar.activation(g_t[:, :], ps[:, Y_BANK, :], ACT.Tanh, scale=0.5).then_inc(y_tanh, 1)

                for kind, t in ORDER[layer][half]:
                    if kind == "unit":
                        a = slot(layer, half, t)
                        act.wait_ge(n["pe_g"], nth(b, half, units, t + 1))
                        if half or t >= 2:
                            act.wait_ge(n["hid_done"], nth(b, half, units, t - 1))
                        nc.scalar.activation(gate[:, a, :], ps[:, 2 * pair_of(layer, half, kind, t), :],
                                             ACT.Tanh if layer else ACT.Silu,
                                             scale=0.5 if layer else 1.0).then_inc(n["gate_act"], 1)
                        if t >= 1:
                            hi(half, t - 1)
                        elif half:
                            hi(0, units - 1)
                        if half and t == 1:
                            experts_out(0)
                        beside.after(t)
                        if next_weights and t >= 3:
                            split_hi(1, t - 3)
                    elif kind == "stack":
                        act.wait_ge(pe_stack, nth(b, half, HG, t + 1))
                        nc.scalar.activation(q_stack[:, t, :], ps[:, 2 * pair_of(layer, half, kind, t), :],
                                             ACT.Copy).then_inc(q_done, 1)
                    elif t < len(STEPS[half]):
                        step, c0 = STEP0[half] + t, first_col(half, STEPS[half][t][1])
                        for p in range(2):
                            act.wait_ge(pe_s, b * (2 * ALL_STEPS) + 2 * step + p + 1)
                            if step >= 2 and p == 0:
                                act.wait_ge(pe_pv, b * ALL_STEPS + step - 1)
                            bank = 2 * pair_of(layer, half, kind, t, p)
                            nc.scalar.activation(prob[:, step % 2, 2 * p:2 * p + 2, c0:CH], ps[:, bank:bank + 2, c0:CH],
                                                 ACT.Exp, scale=HD ** -0.5).then_inc(exp_done, 1)
                if half:
                    hi(1, units - 1)
                    experts_out(1)
                beside.after(units)

            for t in range(U0):
                split_hi(0, t)
            Beside(prelude0(0, 0)).after(U0)
            with act.Fori(0, SEQS - 1) as b:
                chunk(0, b, 0, Beside(prelude0(b, 1)))
                chunk(0, b, 1, Beside(prelude0(b + 1, 0)))
            chunk(0, SEQS - 1, 0, Beside(prelude0(SEQS - 1, 1)))
            chunk(0, SEQS - 1, 1, Beside(prelude1(0, 0)), next_weights=True)
            for t in range(U0 - 3, U1):
                split_hi(1, t)
            with act.Fori(0, SEQS - 1) as b:
                chunk(1, b, 0, Beside(prelude1(b, 1)))
                chunk(1, b, 1, Beside(prelude1(b + 1, 0)))
            chunk(1, SEQS - 1, 0, Beside(prelude1(SEQS - 1, 1)))
            chunk(1, SEQS - 1, 1, Beside())

        @block.vector
        def _(dve):
            state = {"n": 0, "b": 0}

            def link(ins):
                ins.then_inc(v_step, 1)
                state["n"] += 1
                dve.wait_ge(v_step, state["b"] + state["n"])

            def link_alone(ins):
                link(ins)
                dve.sem_inc(waited_dve, 1)

            def norm(src, done, first, second, third):
                yield first
                for t in range(NT):
                    last = nc.vector.bn_stats(stats[:, t, :], src[:, t, :])
                link_alone(last)
                for t in range(NT):
                    last = nc.vector.bn_aggr(mv[:, t, :], stats[:, t, :])
                link(last)
                link(nc.vector.tensor_scalar(var[:, :], mv[:, :, 1], LN_EPS, None, ALU.add))
                yield second
                link(nc.vector.tensor_scalar(rstd[:, 0, :].bitcast(I), var[:, :].bitcast(I), -0.5, 1597463007.0,
                                             ALU.mult, ALU.add))
                for i in range(3):
                    y, y2 = rstd[:, i % 2, :], rstd[:, (i + 1) % 2, :]
                    link(nc.vector.tensor_tensor(newton[:, :], y, y, ALU.mult))
                    if i == 1:
                        yield third
                    link(nc.vector.scalar_tensor_tensor(out=newton[:, :], in0=newton[:, :], scalar=-0.5, in1=var[:, :],
                                                        op0=ALU.mult, op1=ALU.mult))
                    link(nc.vector.scalar_tensor_tensor(out=y2, in0=newton[:, :], scalar=1.5, in1=y,
                                                        op0=ALU.add, op1=ALU.mult))
                nc.vector.scalar_tensor_tensor(out=shift[:, :], in0=mv[:, :, 0], scalar=-1.0, in1=rstd[:, 1, :],
                                               op0=ALU.mult, op1=ALU.mult).then_inc(done, 1)

            def spread(a, n):
                return a.unsqueeze(2).to_broadcast([P, NT, n])

            def bank_rows(bank):
                return ps[:, bank, :].rearrange("p (t d) -> p t d", t=NT)

            def mask_rows(neg, experts, c):
                link(nc.vector.reciprocal(rsum[:, 0, :], rsum[:, 1, :]))
                link(nc.vector.tensor_tensor(neg, neg, spread(rsum[:, 0, :], experts), ALU.mult))
                link(nc.vector.tensor_copy(msk[:, :, 0:experts].bitcast(R), neg))
                nc.vector.tensor_tensor(msk[:, :, experts:2 * experts], neg, msk[:, :, 0:experts],
                                        ALU.subtract).then_inc(c["mask_rows"], 1)

            def prelude0(b, half):
                c = L[0]

                def at(k, per=1):
                    return nth(b, half, per, k)

                def ln2():
                    yield 4
                    dve.wait_ge(c["xn_done"], at(1))
                    yield from norm(xn, c["norm_done"], 4, 5, 7)

                yield 0
                dve.wait_ge(s_xln, 16 * at(1))
                yield from norm(x_ln, c["norm_done"], 0, 1, 2)
                second = Beside(ln2())
                yield 4
                second.after(4)
                yield 5
                second.after(5)
                yield 6
                dve.wait_ge(c["xhi_done"], at(1))
                nc.vector.tensor_tensor(x_lo[:, half, :], ps[:, A_BANK, :], x_hi[:, half, :].bitcast(F),
                                        ALU.subtract).then_inc(c["xlo_done"], 1)
                yield 7
                second.after(7)
                yield 9
                dve.wait_ge(aff_exp, at(1))
                link(nc.vector.tensor_scalar(picked[:, :, :], aff[:, :, :], 1.0, None, ALU.add))
                yield 10
                link_alone(nc.vector.reciprocal(aff[:, :, :], picked[:, :, :]))
                yield 11
                for t in range(NT):
                    last = nc.vector.max(top8[:, t, :], aff[:, t, :])
                link_alone(last)
                yield 12
                dve.wait_ge(v_done, at(1))
                if half:
                    link(nc.vector.tensor_copy(carry[:, :], y_t[:, CH - 1:CH]))
                nc.vector.tensor_tensor_scan(y_t, lam[:, 0:1].to_broadcast([P, CH]), v_t,
                                             carry[:, 0:1] if half else 0.0, ALU.mult, ALU.add).then_inc(y_scan, 1)
                yield 13
                for t in range(NT):
                    last = nc.vector.match_replace(picked[:, t, :], top8[:, t, :], aff[:, t, :], -1.0)
                link(last)
                yield 14
                dve.wait_ge(pe_z, at(1))
                nc.vector.scalar_tensor_tensor(out=z_t, in0=u_t, scalar=vec[:, V_D:V_D + 1], in1=ps[:, B_BANK, :],
                                               op0=ALU.mult, op1=ALU.add).then_inc(z_done, 1)
                yield 15
                link(nc.vector.scalar_tensor_tensor(out=picked[:, :, :], in0=picked[:, :, :], scalar=0.0,
                                                    in1=aff[:, :, :], op0=ALU.max, op1=ALU.subtract))
                link(nc.vector.tensor_reduce(rsum[:, 0, :], picked[:, :, :], AX.X, ALU.add))
                link(nc.vector.tensor_scalar(rsum[:, 1, :], rsum[:, 0, :], -1e-9, None, ALU.add))
                yield 16
                dve.wait_ge(pe_zt, at(1))
                link(nc.vector.tensor_tensor(x2, xn[:, :, :], bank_rows(A_BANK), ALU.add))
                yield from norm(x2, c["norm_done"], 17, 18, 19)
                yield 20
                mask_rows(picked[:, :, :], E0, c)
                yield 28
                dve.wait_ge(pe_z2t, at(1))
                nc.vector.tensor_tensor(s_rows[:, half, :, :], x2, bank_rows(B_BANK), ALU.add).then_inc(s_done, 1)

            def prelude1(b, half):
                c = L[1]

                def at(k, per=1):
                    return nth(b, half, per, k)

                yield 3
                dve.wait_ge(s_xln, 16 * at(1 + CHUNKS))
                yield from norm(x_ln, c["norm_done"], 3, 4, 5)
                yield 8
                dve.wait_ge(c["xhi_done"], at(1))
                nc.vector.tensor_tensor(x_lo[:, half, :], ps[:, A_BANK, :], x_hi[:, half, :].bitcast(F),
                                        ALU.subtract).then_inc(c["xlo_done"], 1)
                yield 14
                dve.wait_ge(c["pe_logits"], at(1))
                lg = aff[:, :, 0:E1]
                link(nc.vector.tensor_tensor(lg, ps[:, A_BANK, 0:NT * E1].rearrange("p (t e) -> p t e", t=NT),
                                             bias_sb[:, :].unsqueeze(1).to_broadcast([P, NT, E1]), ALU.add))
                link(nc.vector.tensor_reduce(rsum[:, 0, :], lg, AX.X, ALU.max))
                nc.vector.tensor_tensor(lg, lg, spread(rsum[:, 0, :], E1), ALU.subtract).then_inc(logit_done, 1)
                yield 15
                dve.wait_ge(score_exp, at(1))
                link(nc.vector.tensor_reduce(rsum[:, 0, :], lg, AX.X, ALU.add))
                link(nc.vector.reciprocal(rsum[:, 1, :], rsum[:, 0, :]))
                link_alone(nc.vector.tensor_tensor(scores1[:, :, 0:E1], lg, spread(rsum[:, 1, :], E1), ALU.mult))
                yield 16
                for t in range(NT):
                    last = nc.vector.max(top8[:, t, :], scores1[:, t, 0:E1])
                link(last)
                link_alone(nc.vector.memset(top8[:, :, 4:8], -1.0))
                yield 17
                for t in range(NT):
                    last = nc.vector.match_replace(aff[:, t, 0:E1 + 4], top8[:, t, :], scores1[:, t, :], -2.0)
                link(last)
                yield 18
                pk = picked[:, :, 0:E1]
                link(nc.vector.scalar_tensor_tensor(out=pk, in0=aff[:, :, 0:E1], scalar=0.0, in1=scores1[:, :, 0:E1],
                                                    op0=ALU.max, op1=ALU.subtract))
                link(nc.vector.tensor_reduce(rsum[:, 0, :], pk, AX.X, ALU.add))
                link(nc.vector.tensor_scalar(rsum[:, 1, :], rsum[:, 0, :], -1e-12, None, ALU.min))
                yield 19
                mask_rows(pk, E1, c)

            def split_lo(layer, t):
                dve.wait_ge(whi_done[layer], t + 1)
                r, _ = staged(layer, t)
                nc.vector.tensor_tensor(w_lo[:, t, :, :].rearrange("p a b -> p (a b)"), stage[:, r, :],
                                        w_hi[:, t, :, :].rearrange("p a b -> p (a b)").bitcast(F),
                                        ALU.subtract).then_inc(wlo_done[layer], 1)

            def chunk(layer, b, half, beside, next_weights=False):
                n, c, units, masked = N[layer], L[layer], UNITS[layer], MASKED[layer]

                def experts_out(half):
                    dve.wait_ge(y_tanh, nth(b, half, 1, 1))
                    nc.vector.scalar_tensor_tensor(out=g_t[:, :], in0=g_t[:, :], scalar=1.0, in1=ps[:, Y_BANK, :],
                                                   op0=ALU.add, op1=ALU.mult).then_inc(c["y_done"], 1)

                def residual(half):
                    dve.wait_ge(c["pe_gt"], nth(b, half, 1, 1))
                    dve.wait_ge(s_xres, 16 * nth(b, half, 1, 1 + layer * CHUNKS))
                    link(nc.vector.scalar_tensor_tensor(
                        out=rows[:, :, :].rearrange("p t d -> p (t d)"),
                        in0=s_rows[:, half, :, :].rearrange("p t d -> p (t d)"), scalar=0.5 if layer else 1.0,
                        in1=ps[:, A_BANK, :], op0=ALU.mult, op1=ALU.mult))
                    nc.vector.tensor_tensor(x_res[:, :, :], x_res[:, :, :], rows[:, :, :], ALU.add).then_inc(c["x_new"], 1)

                def hidden(t):
                    a = slot(layer, half, t)
                    bank = 2 * pair_of(layer, half, "unit", t)
                    g, hd = gate[:, a, :], hid[:, a, :]
                    dve.wait_ge(n["gate_act"], nth(b, half, units, t + 1))
                    if layer:
                        nc.vector.scalar_tensor_tensor(out=g, in0=g, scalar=1.0, in1=ps[:, bank, :], op0=ALU.add,
                                                       op1=ALU.mult).then_inc(n["gate_done"], 1)
                        dve.wait_ge(n["gate_done"], nth(b, half, units, t + 1))
                    dve.wait_ge(n["pe_u"], nth(b, half, units, t + 1))
                    if t < masked:
                        nc.vector.tensor_tensor(g, g, ps[:, bank + 1, :], ALU.mult).then_inc(n["prod_done"], 1)
                        dve.wait_ge(n["prod_done"], nth(b, half, masked, t + 1))
                        dve.wait_ge(n["pe_m"], nth(b, half, masked, t + 1))
                    if half or t >= 2:
                        dve.wait_ge(n["hlo_done"], nth(b, half, units, t - 1))
                    other = ps[:, M_BANK if t < masked else bank + 1, :]
                    if layer:
                        last = nc.vector.scalar_tensor_tensor(out=hd, in0=g, scalar=0.5, in1=other, op0=ALU.mult, op1=ALU.mult)
                    else:
                        last = nc.vector.tensor_tensor(hd, g, other, ALU.mult)
                    last.then_inc(n["hid_done"], 1)

                if layer:
                    dve.wait_ge(c["xn_done"], nth(b, half, 1, 1))
                    nc.vector.tensor_copy(values[:, half * NT:(half + 1) * NT, :, 0:HD],
                                          xn[:, :, :].rearrange("p t (h c) -> p t h c", c=HD)).then_inc(val_done, 1)
                for kind, t in ORDER[layer][half]:
                    if kind == "unit":
                        hidden(t)
                        if layer and half and t == 1:
                            experts_out(0)
                        if half and t == 3:
                            residual(0)
                        beside.after(t)
                        if next_weights and t >= 4:
                            split_lo(1, t - 4)
                    elif kind == "stack":
                        dve.wait_ge(pe_stack, nth(b, half, HG, t + 1))
                        nc.vector.tensor_copy(k_stack[:, t, half * CH:(half + 1) * CH],
                                              ps[:, 2 * pair_of(layer, half, kind, t) + 1, :]).then_inc(k_done, 1)
                    else:
                        if last_of_group(half, t - 1):
                            dve.wait_ge(pe_pv, b * ALL_STEPS + STEP0[half] + t)
                            nc.vector.tensor_copy(heads_out[:, :], ps[:, O_BANK, :]).then_inc(o_done, 1)
                        if last_of_group(half, t - 3):
                            g = STEPS[half][t - 3][0]
                            dve.wait_ge(pe_ot, nth(b, half, HG, g + 1))
                            o = ps[:, A_BANK, :].rearrange("p (t j c) -> p t j c", t=NT, j=4)
                            link(nc.vector.reciprocal(rden[:, :, :], o[:, :, :, HD]))
                            nc.vector.tensor_tensor(
                                s_rows[:, half, :, g * 32:(g + 1) * 32].rearrange("p t (j c) -> p t j c", j=4),
                                o[:, :, :, 0:HD], rden[:, :, :].unsqueeze(3).to_broadcast([P, NT, 4, HD]),
                                ALU.mult).then_inc(so_done, 1)
                if half:
                    if layer:
                        experts_out(1)
                    residual(1)
                beside.after(units)

            dve.wait_ge(s_small, 80)
            nc.vector.memset(scores1[:, :, E1:E1 + 4], -1.0)
            nc.vector.memset(values[:, :, :, HD:VW], 1.0)
            link(nc.vector.tensor_copy(router_hi[:, :], small_sb[:, S_R0:S_END]))
            nc.vector.tensor_tensor(router_lo[:, :], small_sb[:, S_R0:S_END], router_hi[:, :].bitcast(F),
                                    ALU.subtract).then_inc(setup_dve, 1)
            nc.vector.tensor_copy(sel0[:, :].rearrange("p (e i) -> p e i", e=E0),
                                  cst[:, C_OH0:C_OH0 + E0].unsqueeze(2).to_broadcast([P, E0, I0])).then_inc(setup_dve, 1)
            dve.wait_ge(setup_act, 1)
            link(nc.vector.tensor_scalar(lam[:, 1:2], lam[:, 0:1], 1.0, None, ALU.add))
            link(nc.vector.reciprocal(lam[:, 0:1], lam[:, 1:2]))
            nc.vector.tensor_scalar(lam[:, 2:3], lam[:, 0:1], -1.0, 1.0, ALU.mult, ALU.add).then_inc(setup_dve, 1)
            Beside(prelude0(0, 0)).after(U0)

            def sequences(layer, per_sequence, pre):
                before = state["n"]
                with dve.Fori(0, SEQS - 1) as b:
                    state.update(n=before, b=b * per_sequence)
                    chunk(layer, b, 0, Beside(pre(b, 1)))
                    chunk(layer, b, 1, Beside(pre(b + 1, 0)))
                if state["n"] - before != per_sequence:
                    raise ValueError(f"layer {layer}: {state['n'] - before} steps a sequence")
                state.update(n=before + (SEQS - 1) * per_sequence, b=0)

            sequences(0, V0_STEPS, prelude0)
            chunk(0, SEQS - 1, 0, Beside(prelude0(SEQS - 1, 1)))
            chunk(0, SEQS - 1, 1, Beside(prelude1(0, 0)), next_weights=True)
            for t in range(U0 - 4, U1):
                split_lo(1, t)
            sequences(1, V1_STEPS, prelude1)
            chunk(1, SEQS - 1, 0, Beside(prelude1(SEQS - 1, 1)))
            chunk(1, SEQS - 1, 1, Beside())

        @block.gpsimd
        def _(pool):
            def chunk(layer, b, half):
                n, units = N[layer], UNITS[layer]

                def lo(half, t):
                    a = slot(layer, half, t)
                    pool.wait_ge(n["hhi_done"], nth(b, half, units, t + 1))
                    if half or t >= 2:
                        pool.wait_ge(n["pe_down"], nth(b, half, units, t - 1))
                    nc.gpsimd.tensor_tensor(h_lo[:, a, :], hid[:, a, :], h_hi[:, a, :].bitcast(F),
                                            ALU.subtract).then_inc(n["hlo_done"], 1)

                for kind, t in ORDER[layer][half]:
                    if kind == "unit" and t >= 1:
                        lo(half, t - 1)
                    elif kind == "unit" and half:
                        lo(0, units - 1)
                    elif kind == "step" and t < len(STEPS[half]) and diagonal(half, STEPS[half][t][1]):
                        step, c0 = STEP0[half] + t, first_col(half, STEPS[half][t][1])
                        for p in range(2):
                            pool.wait_ge(exp_done, b * (2 * ALL_STEPS) + 2 * step + p + 1)
                            pool.sem_inc(waited_pool, 1)
                            part = prob[:, step % 2, 2 * p:2 * p + 2, c0:c0 + P]
                            nc.gpsimd.affine_select(out=part, in_=part, compare_op=ALU.is_ge, fill=0.0, base=0,
                                                    pattern=[[0, 2], [1, P]], channel_multiplier=-1)\
                                .then_inc(causal_done, 1)
                if half:
                    lo(1, units - 1)

            for t in range(U0):
                pool.wait_ge(whi_done[0], t + 1)
                nc.gpsimd.tensor_tensor(w_lo[:, t, :, :].rearrange("p a b -> p (a b)"), stage[:, t % RING, :],
                                        w_hi[:, t, :, :].rearrange("p a b -> p (a b)").bitcast(F),
                                        ALU.subtract).then_inc(wlo_done[0], 1)
            for layer in range(2):
                with pool.Fori(0, SEQS) as b:
                    for half in range(HALVES):
                        chunk(layer, b, half)

        @block.tensor
        def _(pe):
            mm = nc.tensor.matmul

            def transposes(bank, src, done):
                for t in range(NT):
                    last = nc.tensor.transpose(ps[:, bank, t * P:(t + 1) * P], src(t), ident)
                last.then_inc(done, 1)

            def split3(dst, w0, w1, m0, m1, start, stop):
                mm(dst, w0, m0, start=start, stop=False)
                mm(dst, w0, m1, start=False, stop=False)
                return mm(dst, w1, m0, start=False, stop=stop)

            def logits(experts, c0, half):
                for t in range(NT):
                    dst = ps[:, A_BANK, t * experts:(t + 1) * experts]
                    xs = [a[:, half, t * P:(t + 1) * P] for a in (x_hi, x_lo)]
                    ws = [a[:, c0:c0 + experts] for a in (router_hi, router_lo)]
                    terms = [(x_, w_) for x_ in xs for w_ in ws]
                    for i, (x_, w_) in enumerate(terms):
                        last = mm(dst, x_, w_, start=i == 0, stop=i == 3)
                return last

            a_read = []

            def use_a(reader):
                for waited in a_read:
                    pe.wait_ge(*waited)
                a_read[:] = [reader]

            def prelude0(b, half):
                c = L[0]

                def at(k, per=1):
                    return nth(b, half, per, k)

                yield 5
                pe.wait_ge(c["xn_done"], at(1))
                if not half:
                    x_new = nth(b, half, 1, -1)
                    if not isinstance(x_new, int) or x_new > 0:
                        pe.wait_ge(c["x_new"], x_new)
                transposes(A_BANK, lambda t: xn[:, t, :], c["pe_xt"])
                yield 8
                pe.wait_ge(c["xlo_done"], at(1))
                logits(E0, 0, half).then_inc(c["pe_logits"], 1)
                yield 9
                pe.wait_ge(u0_done, at(1))
                transposes(B_BANK, lambda t: rows[:, t, :], pe_ut)
                yield 11
                pe.wait_ge(aff_exp, at(1))
                pe.wait_ge(u_done, at(1))
                mm(ps[:, A_BANK, :], small_sb[:, S_IN:S_IN + P], u_t, start=True, stop=True).then_inc(pe_up, 1)
                yield 14
                pe.wait_ge(y_scan, at(1))
                mm(ps[:, B_BANK, :], small_sb[:, S_OUT:S_OUT + P], y_t, start=True, stop=True).then_inc(pe_z, 1)
                yield 16
                pe.wait_ge(z_done, at(1))
                transposes(A_BANK, lambda t: z_t[:, t * P:(t + 1) * P], pe_zt)
                yield 21
                pe.wait_ge(h0_done, at(1))
                transposes(B_BANK, lambda t: rows[:, t, :], pe_ht)
                yield 22
                pe.wait_ge(c["mask_rows"], at(1))
                transposes(A_BANK, lambda t: msk[:, t, :], c["pe_mask"])
                yield 24
                pe.wait_ge(c["mask_done"], at(1))
                pe.wait_ge(h_done, at(1))
                for i, bank in enumerate((A_BANK, B_BANK)):
                    mm(ps[:, bank, :], small_sb[:, S_W1 + i * P:S_W1 + (i + 1) * P], v_t,
                       start=True, stop=True).then_inc(pe_f, 1)
                yield 26
                pe.wait_ge(relu_done, at(2, 2))
                for i in range(2):
                    last = mm(ps[:, A_BANK, :], small_sb[:, S_W2 + i * P:S_W2 + (i + 1) * P], relu[:, i, :],
                              start=i == 0, stop=i == 1)
                last.then_inc(pe_z2, 1)
                yield 28
                pe.wait_ge(z2_done, at(1))
                transposes(B_BANK, lambda t: z_t[:, t * P:(t + 1) * P], pe_z2t)

            def prelude1(b, half):
                c = L[1]

                def at(k, per=1):
                    return nth(b, half, per, k)

                yield 7
                pe.wait_ge(c["xn_done"], at(1))
                use_a((c["xlo_done"], at(1)))
                transposes(A_BANK, lambda t: xn[:, t, :], c["pe_xt"])
                yield 14
                use_a((logit_done, at(1)))
                logits(E1, E0, half).then_inc(c["pe_logits"], 1)
                yield 21
                pe.wait_ge(c["mask_rows"], at(1))
                use_a((c["mask_done"], at(1)))
                transposes(A_BANK, lambda t: msk[:, t, :], c["pe_mask"])

            released = []

            def chunk(layer, b, half, beside):
                n, c, units, masked = N[layer], L[layer], UNITS[layer], MASKED[layer]
                if not half:
                    released.clear()

                def pair(kind, t, p, *readers):
                    i = len(released)
                    for waited in released[i - 2] if i >= 2 else ():
                        pe.wait_ge(*waited)
                    released.append(readers)
                    return 2 * pair_of(layer, half, kind, t, p)

                def down(half, t):
                    a = slot(layer, half, t)
                    pe.wait_ge(n["hlo_done"], nth(b, half, units, t + 1))
                    split3(ps[:, Y_BANK, :], w_hi[:, t, 2, :], w_lo[:, t, 2, :], h_hi[:, a, :], h_lo[:, a, :],
                           t == 0, t == units - 1).then_inc(n["pe_down"], 1)

                def gate_rows(half):
                    if layer:
                        use_a((c["x_new"], nth(b, half, 1, 1)))
                    pe.wait_ge(c["y_done"], nth(b, half, 1, 1))
                    transposes(A_BANK, lambda t: g_t[:, t * P:(t + 1) * P], c["pe_gt"])

                def values_product(s):
                    g, k = STEPS[half][s]
                    step, c0 = STEP0[half] + s, first_col(half, k)
                    pe.wait_ge(exp_done, b * (2 * ALL_STEPS) + 2 * step + 2)
                    if diagonal(half, k):
                        pe.wait_ge(causal_done, b * ALL_CAUSAL + causal_after(half, s))
                    if k == 0 and g > 0:
                        pe.wait_ge(o_done, nth(b, half, HG, g))
                    for j in range(4):
                        last = mm(ps[32 * j:32 * j + VW, O_BANK, c0:CH], values[:, k, 4 * g + j, :],
                                  prob[:, step % 2, j, c0:CH], start=k == 0, stop=k == NT * (half + 1) - 1)
                    last.then_inc(pe_pv, 1)

                def rest_of_unit(t):
                    if t == 2 and half:
                        pe.wait_ge(c["y_done"], nth(b, half, 1, 0))
                    if t >= 2:
                        down(half, t - 2)
                    elif half:
                        down(0, units - 2 + t)
                    if t < masked:
                        if t == 0:
                            pe.wait_ge(c["mask_done"], nth(b, half, 1, 1))
                        if half or t >= 1:
                            pe.wait_ge(n["hid_done"], nth(b, half, units, t))
                        if layer == 0:
                            last = mm(ps[:, M_BANK, :], sel0[:, t * P:(t + 1) * P], mask_t[:, half, :], start=True, stop=True)
                        else:
                            last = mm(ps[:, M_BANK, :], onehot1[:, t:t + 1].to_broadcast([2 * E1, P]),
                                      mask_t[0:2 * E1, half, :], start=True, stop=True)
                        last.then_inc(n["pe_m"], 1)
                    if half and t == 2:
                        gate_rows(0)
                    beside.after(t)

                xh, xl = x_hi[:, half, :], x_lo[:, half, :]
                rest = None
                for kind, t in ORDER[layer][half]:
                    if rest is not None and (kind != "step" or t >= len(STEPS[half])):
                        rest_of_unit(rest)
                        rest = None
                    if kind == "unit":
                        if not half:
                            pe.wait_ge(wlo_done[layer], t + 1)
                        reader = (n["prod_done"], nth(b, half, masked, t + 1)) if t < masked else \
                            (n["hid_done"], nth(b, half, units, t + 1))
                        bank = pair(kind, t, 0, reader)
                        split3(ps[:, bank, :], w_hi[:, t, 0, :], w_lo[:, t, 0, :], xh, xl, True, True).then_inc(n["pe_g"], 1)
                        split3(ps[:, bank + 1, :], w_hi[:, t, 1, :], w_lo[:, t, 1, :], xh, xl, True, True).then_inc(n["pe_u"], 1)
                        rest = t
                    elif kind == "stack":
                        if t == 0:
                            pe.wait_ge(val_done, nth(b, half, 1, 1))
                        bank = pair(kind, t, 0, (q_done, nth(b, half, HG, t + 1)), (k_done, nth(b, half, HG, t + 1)))
                        r = slice(32 * t, 32 * t + 32)
                        for which in range(2):
                            mm(ps[:, bank + which, :], sel[r, 2 * which, :], xh[r, :], start=True, stop=False)
                            last = mm(ps[:, bank + which, :], sel[r, 2 * which + 1, :], xl[r, :], start=False, stop=True)
                        last.then_inc(pe_stack, 1)
                    else:
                        if t < len(STEPS[half]):
                            g, k = STEPS[half][t]
                            step, c0 = STEP0[half] + t, first_col(half, k)
                            if k == 0:
                                pe.wait_ge(q_done, nth(b, half, HG, g + 1))
                                pe.wait_ge(k_done, nth(b, half, HG, g + 1))
                            for p in range(2):
                                if p == 1:
                                    if rest is not None:
                                        rest_of_unit(rest)
                                        rest = None
                                    if t >= 1:
                                        values_product(t - 1)
                                bank = pair(kind, t, p, (exp_done, b * (2 * ALL_STEPS) + 2 * step + p + 1))
                                for j in (2 * p, 2 * p + 1):
                                    r = slice(32 * j, 32 * j + 32)
                                    last = mm(ps[:, bank + j % 2, c0:CH], k_stack[r, g, k * P:(k + 1) * P],
                                              q_stack[r, g, c0:CH], start=True, stop=True)
                                last.then_inc(pe_s, 1)
                        if t == len(STEPS[half]):
                            values_product(t - 1)
                        if last_of_group(half, t - 2):
                            g = STEPS[half][t - 2][0]
                            pe.wait_ge(o_done, nth(b, half, HG, g + 1))
                            use_a((so_done, nth(b, half, HG, g + 1)))
                            transposes(A_BANK, lambda t: heads_out[:, t * P:(t + 1) * P], pe_ot)
                if rest is not None:
                    rest_of_unit(rest)
                if half:
                    down(1, units - 2)
                    down(1, units - 1)
                    gate_rows(1)
                beside.after(units)

            pe.wait_ge(s_small, 80)
            pe.wait_ge(setup_dve, 3)
            Beside(prelude0(0, 0)).after(U0)
            with pe.Fori(0, SEQS - 1) as b:
                chunk(0, b, 0, Beside(prelude0(b, 1)))
                chunk(0, b, 1, Beside(prelude0(b + 1, 0)))
            chunk(0, SEQS - 1, 0, Beside(prelude0(SEQS - 1, 1)))
            a_read[:] = [(L[0]["x_new"], CHUNKS - 1)]
            chunk(0, SEQS - 1, 1, Beside(prelude1(0, 0)))
            pe.wait_ge(setup_act, 3)
            a_read.clear()
            with pe.Fori(0, SEQS - 1) as b:
                chunk(1, b, 0, Beside(prelude1(b, 1)))
                chunk(1, b, 1, Beside(prelude1(b + 1, 0)))
                a_read.clear()
            chunk(1, SEQS - 1, 0, Beside(prelude1(SEQS - 1, 1)))
            chunk(1, SEQS - 1, 1, Beside())


def _pairs():
    table = {}
    for layer, orders in enumerate(((ORDER0, ORDER0), ORDER1)):
        i = 0
        for half, order in enumerate(orders):
            for kind, t in order:
                uses = 0 if kind == "step" and t >= len(STEPS[half]) else 2 if kind == "step" else 1
                for p in range(uses):
                    table[layer, half, kind, t, p] = i % 2
                    i += 1
        assert i % 2 == 0
    return table


PAIRS = _pairs()


def pair_of(layer, half, kind, t, p=0):
    return PAIRS[layer, half, kind, t, p]


def _units(parts, units):
    import numpy as np
    w = np.zeros((units, P, 3, P), np.float32)
    for at, n, gate_, up_, down_ in parts:
        w[at:at + n, :, 0, :gate_.shape[2]] = gate_
        w[at:at + n, :, 1, :up_.shape[2]] = up_
        w[at:at + n, :down_.shape[1], 2, :] = down_
    return w.reshape(units, P, 3 * P)


def _constants():
    import numpy as np
    c = np.zeros((P, C_END), np.float32)
    k = np.arange(P)
    c[k, C_ID + k] = 1.0
    c[k, C_OH0 + k % E0] = 1.0
    c[k, C_OH1 + k % E1] = 1.0
    for n, slots in enumerate(((0, 1), (2, 3), (0, 2), (1, 3))):
        for a in slots:
            r = k % 32
            c[k, C_SEL + n * P + 32 * (r // 8) + 8 * a + r % 8] = 1.0
    return c


def kernel(**inputs):
    import numpy as np
    import concourse.bacc as bacc
    from concourse.bass_utils import run_bass_kernel_spmd

    a = {k: np.asarray(v) for k, v in inputs.items()}

    def pairs(w):
        return w.reshape(M0, 2, P, I0).transpose(0, 2, 1, 3).reshape(M0, P, P)

    w0 = _units([
        (0, M0, pairs(a["L0_ffn_expert_gate_k"]), pairs(a["L0_ffn_expert_up_k"]), a["L0_ffn_expert_down_k"].reshape(M0, P, D)),
        (M0, 1, a["L0_ffn_shared_gate_w"][None], a["L0_ffn_shared_up_w"][None], a["L0_ffn_shared_down_w"][None]),
    ], U0)
    S = U1 - M1
    w1 = _units([
        (0, M1, *(a[f"L1_ffn_{n}_w"].transpose(0, 2, 1) for n in ("gate", "up", "down"))),
        (M1, S, *(a[f"L1_ffn_{n}_w"].reshape(S, P, D).transpose(0, 2, 1) for n in ("sgate", "sup")),
         a["L1_ffn_sdown_w"].T.reshape(S, P, D)),
    ], U1)
    small = np.concatenate([
        a["L0_attn_w_in"].T, a["L0_attn_w_out"].T, a["L0_attn_w1"].T,
        a["L0_attn_w2"].T.reshape(2, P, D).transpose(1, 0, 2).reshape(P, 2 * D),
        a["L0_ffn_router_w"], a["L1_ffn_router_w"].T], axis=1)
    vectors = np.stack([a["L0_attn_log_lambda"], a["L0_attn_D_skip"], a["L0_attn_ln1_g"], a["L0_attn_ln1_b"],
                        a["L0_attn_ln2_g"], a["L0_attn_ln2_b"], a["L0_attn_b1"][:P], a["L0_attn_b1"][P:],
                        a["L0_attn_b2"]], axis=1)
    arrays = {
        "x_dram": a["L0_attn_x"].reshape(SEQS * T, D), "weights0_dram": w0, "weights1_dram": w1,
        "small_dram": small, "vectors_dram": vectors, "bias1_dram": a["L1_ffn_router_bias"],
        "constants_dram": _constants(),
    }
    arrays = {k: np.ascontiguousarray(v) for k, v in arrays.items()}
    nc = bacc.Bacc("TRN2", target_bir_lowering=False, num_devices=1, dynamic_dma_scratch_size=1024)
    args = [nc.dram_tensor(k, v.shape, mybir.dt.from_np(v.dtype), kind="ExternalInput").ap() for k, v in arrays.items()]
    out = nc.dram_tensor("out_dram", (SEQS * T, D), mybir.dt.float32, kind="ExternalOutput").ap()
    x1 = nc.dram_tensor("x1_dram", (SEQS * T, D), mybir.dt.float32, kind="Internal").ap()
    two_layers(nc, *args, x1, out)
    r = run_bass_kernel_spmd(nc, [arrays], core_ids=[0])
    return r.results[0]["out_dram"].reshape(SEQS, T, D)
```

```python
import concourse.bass as bass
from concourse import mybir
from contextlib import ExitStack

P = 128
SEQS, T, D = 4, 1024, 128
CH = 512
NT = CH // P
HALVES = T // CH
CHUNKS = SEQS * HALVES
TILES = SEQS * T // P
E0, I0 = 64, 64
E1 = 32
M0 = E0 * I0 // P
M1 = E1
U0 = M0 + 1
U1 = M1 + 4
HEADS, HD = 16, 8
HG = HEADS // 4
VW = HD + 1
LN_EPS = 1e-5
RING = 4
LAG = 3
AHEAD = 12

C_ID, C_OH0, C_OH1, C_SEL = 0, 128, 192, 224
C_END = 224 + 4 * P
V_LL, V_D, V_G1, V_B1, V_G2, V_B2, V_FB, V_B = 0, 1, 2, 3, 4, 5, 6, 8
V_END = 9
S_IN, S_OUT, S_W1, S_W2, S_R0, S_R1 = 0, 128, 256, 512, 768, 832
S_END = 864

M_BANK, Y_BANK = 4, 5
A_BANK, B_BANK, O_BANK = 6, 7, 7

LN_STEPS = 13
PRE0_STEPS = 3 * LN_STEPS + 11
PRE1_STEPS = LN_STEPS + 14
V0_STEPS = HALVES * PRE0_STEPS + 1
V1_STEPS = HALVES * (PRE1_STEPS + HG)

STEPS = [[(g, k) for g in range(HG) for k in range(NT * (half + 1))] for half in range(HALVES)]
STEP0 = [0, len(STEPS[0])]
ALL_STEPS = len(STEPS[0]) + len(STEPS[1])
TAIL = 3


def order1(half):
    entries, s, total = [], 0, len(STEPS[half]) + TAIL
    start = 2 if half else 3
    for t in range(U1):
        if t < HG:
            entries.append(("stack", t))
        entries.append(("unit", t))
        while s < total and s * max(U1 - 1 - start, total) < (t - start) * total:
            entries.append(("step", s))
            s += 1
    while s < total:
        entries.append(("step", s))
        s += 1
    return entries


ORDER1 = [order1(half) for half in range(HALVES)]
ORDER0 = [("unit", t) for t in range(U0)]


class Beside:

    def __init__(self, parts=iter(())):
        self.parts = parts
        self.due = next(parts, None)

    def after(self, unit):
        while self.due is not None and self.due <= unit:
            self.due = next(self.parts, None)


FIRST_PART = 19
CATCH_UP = 3


class CatchUp:

    def __init__(self, own, following):
        self.own, self.following = own, following

    def after(self, unit):
        if unit < CATCH_UP:
            self.own.after(FIRST_PART + (unit + 1) * (U0 - FIRST_PART) // CATCH_UP)
        else:
            self.following.after(unit if unit == U0 else (unit - CATCH_UP + 1) * U0 // (U0 - CATCH_UP))


def two_layers(nc, x, weights0, weights1, small, vectors, bias1, constants, x1, out):
    F, R, I = mybir.dt.float32, mybir.dt.float32r, mybir.dt.int32
    ALU, ACT, AX = mybir.AluOpType, mybir.ActivationFunctionType, mybir.AxisListType
    ctx = ExitStack()
    with ctx:
        def sb(name, shape, dt=F):
            return ctx.enter_context(nc.sbuf_tensor(name, shape, dt))

        def sem(name):
            return ctx.enter_context(nc.semaphore(name))

        x_ln = sb("x_ln", [P, NT, D])
        x_res = sb("x_res", [P, NT, D])
        w_hi = sb("w_hi", [P, U1, 3, P], R)
        w_lo = sb("w_lo", [P, U1, 3, P], R)
        stage = sb("stage", [P, RING, 3 * P])
        x_hi = sb("x_hi", [P, 2, CH], R)
        x_lo = sb("x_lo", [P, 2, CH], R)
        h_hi = sb("h_hi", [P, LAG, CH], R)
        h_lo = sb("h_lo", [P, LAG, CH], R)
        mask_t = sb("mask_t", [P, 2, CH], R)
        router_hi = sb("router_hi", [P, E0 + E1], R)
        router_lo = sb("router_lo", [P, E0 + E1], R)
        onehot1 = sb("onehot1", [2 * E1, E1], R)
        sel = sb("sel", [P, 4, P], R)
        sel0_keys = sb("sel0_keys", [P, E0 * I0], R)
        sel0 = sel0_keys
        k_stack = sel0_keys[:, :].rearrange("p (g t) -> p g t", g=HG)
        q_stack = sb("q_stack", [P, HG, CH], R)
        gate = sb("gate", [P, 2, CH])
        hid = sb("hid", [P, 2, CH])
        work = sb("work", [P, 8 * CH])
        relu = work[:, 0:2 * CH].rearrange("p (a t) -> p a t", a=2)
        u_t, v_t, y_t, z_t, x2_flat = (work[:, i * CH:(i + 1) * CH] for i in range(2, 7))
        x2 = x2_flat.rearrange("p (t d) -> p t d", t=NT)
        prob = work[:, :].rearrange("p (a j t) -> p a j t", a=2, j=4)
        values = sb("values", [P, HALVES * NT, HEADS, VW])
        xn = sb("xn", [P, NT, D])
        rows = sb("rows", [P, NT, D])
        g_t = sb("g_t", [P, CH])
        heads_out = sel_raw = g_t
        s_rows = sb("s_rows", [P, 2, NT, D])
        msk = sb("msk", [P, NT, P])
        small_sb = sb("small_sb", [P, S_END])
        vec = sb("vec", [P, V_END])
        cst = sb("cst", [P, C_SEL])
        bias_sb = sb("bias_sb", [P, E1])
        lam = sb("lam", [P, 3])
        carry = sb("carry", [P, 1])
        stats = sb("stats", [P, NT, 6])
        mv = sb("mv", [P, NT, 2])
        var = sb("var", [P, NT])
        rstd = sb("rstd", [P, 2, NT])
        newton = sb("newton", [P, NT])
        shift = sb("shift", [P, NT])
        aff = sb("aff", [P, NT, E0])
        scores1 = sb("scores1", [P, NT, E1 + 4])
        picked = sb("picked", [P, NT, E0])
        top8 = sb("top8", [P, NT, 8])
        rsum = sb("rsum", [P, 2, NT])
        rden = sb("rden", [P, NT, 4])
        ident = cst[:, C_ID:C_ID + P]

        ps = ctx.enter_context(nc.psum_tensor("ps", [P, 8, 512], F))

        s_small, s_xln, s_xres = sem("s_small"), sem("s_xln"), sem("s_xres")
        s_stage = [sem(f"s_stage{i}") for i in range(RING)]
        s_store = [sem("s_store0"), sem("s_store1")]
        whi_done = [sem("whi_done0"), sem("whi_done1")]
        wlo_done = [sem("wlo_done0"), sem("wlo_done1")]
        setup_act, setup_dve = sem("setup_act"), sem("setup_dve")
        v_step = sem("v_step")
        waited_dve, waited_pool, waited_sp = map(sem, ("waited_dve", "waited_pool", "waited_sp"))
        names = ("norm_done xn_done pe_xt xhi_done xlo_done pe_logits pe_mask mask_rows mask_done "
                 "y_done pe_gt gated x_new").split()
        L = [{n: sem(f"{n}{i}") for n in names} for i in range(2)]
        unit = "pe_g pe_u pe_m gate_act gate_done prod_done hid_done hhi_done hlo_done pe_down".split()
        N = [{n: sem(f"{n}{i}") for n in unit} for i in range(2)]
        u0_done, pe_ut, u_done, pe_up, v_done, y_scan = map(sem, "u0_done pe_ut u_done pe_up v_done y_scan".split())
        pe_z, z_done, pe_zt, h0_done, pe_ht, h_done = map(sem, "pe_z z_done pe_zt h0_done pe_ht h_done".split())
        pe_f, relu_done, pe_z2, z2_done, pe_z2t, s_done = map(sem, "pe_f relu_done pe_z2 z2_done pe_z2t s_done".split())
        aff_exp = sem("aff_exp")
        logit_done, score_exp, val_done, y_tanh = map(sem, "logit_done score_exp val_done y_tanh".split())
        pe_stack, q_done, k_done = sem("pe_stack"), sem("q_done"), sem("k_done")
        pe_s, exp_done, causal_done = sem("pe_s"), sem("exp_done"), sem("causal_done")
        pe_pv, o_done, pe_ot, so_done = sem("pe_pv"), sem("o_done"), sem("pe_ot"), sem("so_done")

        def nth(b, half, per_chunk, k):
            return b * (HALVES * per_chunk) + (half * per_chunk + k)

        def first_col(half, k):
            return max(k - NT * half, 0) * P

        def diagonal(half, k):
            return k >= NT * half

        def causal_after(half, s):
            before = 2 * sum(diagonal(0, k) for _, k in STEPS[0]) * half
            return before + 2 * sum(diagonal(half, k) for _, k in STEPS[half][:s + 1])

        ALL_CAUSAL = causal_after(1, len(STEPS[1]) - 1)

        def last_of_group(half, s):
            return 0 <= s < len(STEPS[half]) and STEPS[half][s][1] == NT * (half + 1) - 1

        UNITS, MASKED, ORDER = (U0, U1), (M0, M1), ((ORDER0, ORDER0), ORDER1)

        def slot(layer, half, t):
            return (half * UNITS[layer] + t) % 2

        def part_slot(layer, half, t):
            return (half * UNITS[layer] + t) % LAG

        STAGE_USES = [(U0 + RING - 1 - r) // RING for r in range(RING)]

        def staged(layer, t):
            r = (t + layer * U0) % RING
            return r, 16 * (t // RING + 1) if not layer else 16 * ((t + U0) // RING + 1)

        block = ctx.enter_context(nc.Block())

        @block.sync
        def _(sp):
            def tiles(dram, b, half):
                return dram.rearrange("(t p) d -> p t d", p=P)[:, bass.ds(b * (2 * NT) + half * NT, NT), :]

            def load_ln(src, b, half):
                sp.dma_start(x_ln[:, :, :], tiles(src, b, half)).then_inc(s_xln, 16)

            def load_units(layer, src, first=0, end=None):
                for t in range(first, end or UNITS[layer]):
                    if t >= RING:
                        sp.wait_ge(wlo_done[layer], t - RING + 1)
                    elif layer:
                        sp.wait_ge(wlo_done[0], U0 - RING + t + 1)
                    r, _ = staged(layer, t)
                    sp.dma_start(stage[:, r, :], src[t, :, :]).then_inc(s_stage[r], 16)

            def wait_alone(semaphore, count):
                sp.wait_ge(semaphore, count)
                sp.sem_inc(waited_sp, 1)

            def load_res(src, b, half):
                sp.dma_start(x_res[:, :, :], tiles(src, b, half)).then_inc(s_xres, 16)

            def next_ln(layer, b, half, src, next_b, next_half):
                wait_alone(L[layer]["xn_done"], nth(b, half, 1, 1))
                load_ln(src, next_b, next_half)

            def store(layer, b, half, dst):
                wait_alone(L[layer]["x_new"], nth(b, half, 1, 1))
                sp.dma_start(tiles(dst, b, half), x_res[:, :, :]).then_inc(s_store[layer], 16)
                wait_alone(s_store[layer], 16 * nth(b, half, 1, 1))

            def rows(layer, src, dst, last_loads, units):
                load_res(src, 0, 0)
                with sp.Fori(0, SEQS - 1) as b:
                    next_ln(layer, b, 1, src, b + 1, 0)
                    store(layer, b, 0, dst)
                    load_res(src, b, 1)
                    next_ln(layer, b + 1, 0, src, b + 1, 1)
                    store(layer, b, 1, dst)
                    load_res(src, b + 1, 0)
                last_loads()
                store(layer, SEQS - 1, 0, dst)
                load_res(src, SEQS - 1, 1)
                units()
                store(layer, SEQS - 1, 1, dst)

            load_ln(x, 0, 0)
            sp.dma_start(cst[:, :], constants[:, 0:C_SEL]).then_inc(s_small, 16)
            sp.dma_start(vec[:, :], vectors).then_inc(s_small, 16)
            sp.dma_start(sel_raw[:, :], constants[:, C_SEL:C_END]).then_inc(s_small, 16)
            sp.dma_start(small_sb[:, :], small).then_inc(s_small, 16)
            sp.dma_start(bias_sb[:, :], bias1.partition_broadcast(P)).then_inc(s_small, 16)
            load_units(0, weights0, 0, AHEAD)
            next_ln(0, 0, 0, x, 0, 1)
            load_units(0, weights0, AHEAD)
            def layer1_loads():
                load_units(1, weights1, 0, U1 // 2)
                next_ln(1, 0, 0, x1, 0, 1)
                load_units(1, weights1, U1 // 2)

            rows(0, x, x1, lambda: next_ln(0, SEQS - 1, 1, x1, 0, 0), layer1_loads)
            rows(1, x1, out, lambda: None, lambda: None)

        @block.scalar
        def _(act):
            act.wait_ge(s_small, 80)
            nc.scalar.activation(lam[:, 0:1], vec[:, V_LL:V_LL + 1], ACT.Exp, scale=-1.0).then_inc(setup_act, 1)
            nc.scalar.activation(sel[:, :, :].rearrange("p a b -> p (a b)"), sel_raw[:, :], ACT.Copy).then_inc(setup_act, 1)
            nc.scalar.activation(onehot1[:, :], cst[0:2 * E1, C_OH1:C_OH1 + E1], ACT.Copy).then_inc(setup_act, 1)

            def split_hi(layer, t):
                r, count = staged(layer, t)
                act.wait_ge(s_stage[r], count)
                if layer and t < U0:
                    act.wait_ge(N[0]["pe_down"], nth(SEQS - 1, 1, U0, t + 1))
                nc.scalar.activation(w_hi[:, t, :, :].rearrange("p a b -> p (a b)"), stage[:, r, :],
                                     ACT.Copy).then_inc(whi_done[layer], 1)

            def splits(layer, ahead):
                return lambda t: split_hi(layer, t + ahead) if 0 <= t + ahead < UNITS[layer] else None

            def normalise(src, dst, done):
                for t in range(NT):
                    last = nc.scalar.activation(dst[:, t, :], src[:, t, :], ACT.Identity, bias=shift[:, t:t + 1],
                                                scale=rstd[:, 1, t:t + 1])
                last.then_inc(done, 1)

            def prelude0(b, half):
                c = L[0]

                def at(k, per=1):
                    return nth(b, half, per, k)

                yield 3
                act.wait_ge(c["norm_done"], at(1, 3))
                normalise(x_ln, xn, c["xn_done"])
                yield 7
                act.wait_ge(c["pe_xt"], at(1))
                nc.scalar.activation(x_hi[:, half, :], ps[:, A_BANK, :], ACT.Copy).then_inc(c["xhi_done"], 1)
                yield 9
                act.wait_ge(c["norm_done"], at(2, 3))
                x_new = nth(b, half, 1, -1)
                if not isinstance(x_new, int) or x_new > 0:
                    act.wait_ge(c["x_new"], x_new)
                normalise(xn, rows, u0_done)
                yield 10
                act.wait_ge(c["pe_logits"], at(1))
                nc.scalar.activation(aff[:, :, :].rearrange("p t e -> p (t e)"), ps[:, A_BANK, 0:NT * E0], ACT.Exp,
                                     scale=-1.0).then_inc(aff_exp, 1)
                yield 11
                act.wait_ge(pe_ut, at(1))
                nc.scalar.activation(u_t, ps[:, B_BANK, :], ACT.Identity, bias=vec[:, V_B1:V_B1 + 1],
                                     scale=vec[:, V_G1:V_G1 + 1]).then_inc(u_done, 1)
                yield 13
                act.wait_ge(pe_up, at(1))
                nc.scalar.activation(v_t, ps[:, A_BANK, :], ACT.Copy, scale=lam[:, 2:3]).then_inc(v_done, 1)
                yield 19
                act.wait_ge(c["pe_mask"], at(1))
                nc.scalar.activation(mask_t[:, half, :], ps[:, A_BANK, :], ACT.Copy).then_inc(c["mask_done"], 1)
                yield 24
                act.wait_ge(c["norm_done"], at(3, 3))
                normalise(x2, rows, h0_done)
                yield 26
                act.wait_ge(pe_ht, at(1))
                nc.scalar.activation(v_t, ps[:, B_BANK, :], ACT.Identity, bias=vec[:, V_B2:V_B2 + 1],
                                     scale=vec[:, V_G2:V_G2 + 1]).then_inc(h_done, 1)
                yield 28
                for i, bank in enumerate((A_BANK, B_BANK)):
                    act.wait_ge(pe_f, at(i + 1, 2))
                    nc.scalar.activation(relu[:, i, :], ps[:, bank, :], ACT.Relu,
                                         bias=vec[:, V_FB + i:V_FB + i + 1]).then_inc(relu_done, 1)
                yield 30
                act.wait_ge(pe_z2, at(1))
                nc.scalar.activation(z_t, ps[:, A_BANK, :], ACT.Identity, bias=vec[:, V_B:V_B + 1]).then_inc(z2_done, 1)

            def prelude1(b, half):
                c = L[1]

                def at(k, per=1):
                    return nth(b, half, per, k)

                yield 8
                act.wait_ge(c["norm_done"], at(1))
                normalise(x_ln, xn, c["xn_done"])
                yield 9
                act.wait_ge(c["pe_xt"], at(1))
                nc.scalar.activation(x_hi[:, half, :], ps[:, A_BANK, :], ACT.Copy).then_inc(c["xhi_done"], 1)
                yield 16
                act.wait_ge(logit_done, at(1))
                nc.scalar.activation(aff[:, :, 0:E1], aff[:, :, 0:E1], ACT.Exp).then_inc(score_exp, 1)
                yield 23
                act.wait_ge(c["pe_mask"], at(1))
                nc.scalar.activation(mask_t[0:2 * E1, half, :], ps[0:2 * E1, A_BANK, :], ACT.Copy).then_inc(c["mask_done"], 1)

            def chunk(layer, b, half, beside, first=False, final=False, split=None):
                n, c, units = N[layer], L[layer], UNITS[layer]

                def hi(t):
                    a, to = slot(layer, half, t), part_slot(layer, half, t)
                    act.wait_ge(n["hid_done"], nth(b, half, units, t + 1))
                    if not first or t >= LAG:
                        act.wait_ge(n["pe_down"], nth(b, half, units, t + 1 - LAG))
                    nc.scalar.activation(h_hi[:, to, :], hid[:, a, :], ACT.Copy).then_inc(n["hhi_done"], 1)

                def experts_out(k):
                    act.wait_ge(n["pe_down"], nth(b, half, units, k * units))
                    if layer == 0:
                        nc.scalar.activation(g_t[:, :], ps[:, Y_BANK, :], ACT.Silu).then_inc(c["y_done"], 1)
                    else:
                        nc.scalar.activation(g_t[:, :], ps[:, Y_BANK, :], ACT.Tanh, scale=0.5).then_inc(y_tanh, 1)

                for kind, t in ORDER[layer][half]:
                    if kind == "unit":
                        a = slot(layer, half, t)
                        act.wait_ge(n["pe_g"], nth(b, half, units, t + 1))
                        if not first or t >= 2:
                            act.wait_ge(n["hid_done"], nth(b, half, units, t - 1))
                        nc.scalar.activation(gate[:, a, :], ps[:, 2 * pair_of(layer, half, kind, t), :],
                                             ACT.Tanh if layer else ACT.Silu,
                                             scale=0.5 if layer else 1.0).then_inc(n["gate_act"], 1)
                        if not first or t >= 1:
                            hi(t - 1)
                        if not first and t == LAG - 1:
                            experts_out(0)
                        beside.after(t)
                        if split is not None:
                            split(t)
                    elif kind == "stack":
                        act.wait_ge(pe_stack, nth(b, half, HG, t + 1))
                        nc.scalar.activation(q_stack[:, t, :], ps[:, 2 * pair_of(layer, half, kind, t), :],
                                             ACT.Copy).then_inc(q_done, 1)
                    elif t < len(STEPS[half]):
                        step, c0 = STEP0[half] + t, first_col(half, STEPS[half][t][1])
                        for p in range(2):
                            act.wait_ge(pe_s, b * (2 * ALL_STEPS) + 2 * step + p + 1)
                            if (not first or t >= 2) and p == 0:
                                act.wait_ge(pe_pv, b * ALL_STEPS + step - 1)
                            bank = 2 * pair_of(layer, half, kind, t, p)
                            nc.scalar.activation(prob[:, step % 2, 2 * p:2 * p + 2, c0:CH], ps[:, bank:bank + 2, c0:CH],
                                                 ACT.Exp, scale=HD ** -0.5).then_inc(exp_done, 1)
                if final:
                    hi(units - 1)
                    experts_out(1)
                beside.after(units)

            first_prelude = Beside(prelude0(0, 0))
            for t in range(AHEAD):
                split_hi(0, t)
                first_prelude.after(min(3 * t, FIRST_PART))
            first_prelude.after(FIRST_PART)
            chunk(0, 0, 0, CatchUp(first_prelude, Beside(prelude0(0, 1))), first=True, split=splits(0, AHEAD))
            with act.Fori(0, SEQS - 1) as b:
                chunk(0, b, 1, Beside(prelude0(b + 1, 0)))
                chunk(0, b + 1, 0, Beside(prelude0(b + 1, 1)))
            chunk(0, SEQS - 1, 1, Beside(prelude1(0, 0)), final=True, split=splits(1, -8))
            chunk(1, 0, 0, Beside(prelude1(0, 1)), first=True, split=splits(1, U0 - 8))
            with act.Fori(0, SEQS - 1) as b:
                chunk(1, b, 1, Beside(prelude1(b + 1, 0)))
                chunk(1, b + 1, 0, Beside(prelude1(b + 1, 1)))
            chunk(1, SEQS - 1, 1, Beside(), final=True)

        @block.vector
        def _(dve):
            state = {"n": 0, "b": 0}

            def link(ins):
                ins.then_inc(v_step, 1)
                state["n"] += 1
                dve.wait_ge(v_step, state["b"] + state["n"])

            def link_alone(ins):
                link(ins)
                dve.sem_inc(waited_dve, 1)

            def norm(src, done, first, second, third):
                yield first
                for t in range(NT):
                    last = nc.vector.bn_stats(stats[:, t, :], src[:, t, :])
                link_alone(last)
                for t in range(NT):
                    last = nc.vector.bn_aggr(mv[:, t, :], stats[:, t, :])
                link(last)
                link(nc.vector.tensor_scalar(var[:, :], mv[:, :, 1], LN_EPS, None, ALU.add))
                yield second
                link(nc.vector.tensor_scalar(rstd[:, 0, :].bitcast(I), var[:, :].bitcast(I), -0.5, 1597463007.0,
                                             ALU.mult, ALU.add))
                for i in range(3):
                    y, y2 = rstd[:, i % 2, :], rstd[:, (i + 1) % 2, :]
                    link(nc.vector.tensor_tensor(newton[:, :], y, y, ALU.mult))
                    if i == 1:
                        yield third
                    link(nc.vector.scalar_tensor_tensor(out=newton[:, :], in0=newton[:, :], scalar=-0.5, in1=var[:, :],
                                                        op0=ALU.mult, op1=ALU.mult))
                    link(nc.vector.scalar_tensor_tensor(out=y2, in0=newton[:, :], scalar=1.5, in1=y,
                                                        op0=ALU.add, op1=ALU.mult))
                nc.vector.scalar_tensor_tensor(out=shift[:, :], in0=mv[:, :, 0], scalar=-1.0, in1=rstd[:, 1, :],
                                               op0=ALU.mult, op1=ALU.mult).then_inc(done, 1)

            def spread(a, n):
                return a.unsqueeze(2).to_broadcast([P, NT, n])

            def bank_rows(bank):
                return ps[:, bank, :].rearrange("p (t d) -> p t d", t=NT)

            def mask_rows(neg, experts, c):
                link(nc.vector.reciprocal(rsum[:, 0, :], rsum[:, 1, :]))
                link(nc.vector.tensor_tensor(neg, neg, spread(rsum[:, 0, :], experts), ALU.mult))
                link(nc.vector.tensor_copy(msk[:, :, 0:experts].bitcast(R), neg))
                nc.vector.tensor_tensor(msk[:, :, experts:2 * experts], neg, msk[:, :, 0:experts],
                                        ALU.subtract).then_inc(c["mask_rows"], 1)

            def prelude0(b, half):
                c = L[0]

                def at(k, per=1):
                    return nth(b, half, per, k)

                def ln2():
                    yield 5
                    dve.wait_ge(c["xn_done"], at(1))
                    yield from norm(xn, c["norm_done"], 5, 6, 8)

                yield 0
                dve.wait_ge(s_xln, 16 * at(1))
                yield from norm(x_ln, c["norm_done"], 0, 1, 2)
                second = Beside(ln2())
                yield 5
                second.after(5)
                yield 6
                second.after(6)
                yield 7
                dve.wait_ge(c["xhi_done"], at(1))
                nc.vector.tensor_tensor(x_lo[:, half, :], ps[:, A_BANK, :], x_hi[:, half, :].bitcast(F),
                                        ALU.subtract).then_inc(c["xlo_done"], 1)
                yield 8
                second.after(8)
                yield 10
                dve.wait_ge(aff_exp, at(1))
                link(nc.vector.tensor_scalar(picked[:, :, :], aff[:, :, :], 1.0, None, ALU.add))
                yield 11
                link_alone(nc.vector.reciprocal(aff[:, :, :], picked[:, :, :]))
                yield 12
                for t in range(NT):
                    last = nc.vector.max(top8[:, t, :], aff[:, t, :])
                link_alone(last)
                yield 13
                for t in range(NT):
                    last = nc.vector.match_replace(picked[:, t, :], top8[:, t, :], aff[:, t, :], -1.0)
                link(last)
                yield 14
                dve.wait_ge(v_done, at(1))
                if half:
                    link(nc.vector.tensor_copy(carry[:, :], y_t[:, CH - 1:CH]))
                nc.vector.tensor_tensor_scan(y_t, lam[:, 0:1].to_broadcast([P, CH]), v_t,
                                             carry[:, 0:1] if half else 0.0, ALU.mult, ALU.add).then_inc(y_scan, 1)
                yield 15
                link(nc.vector.scalar_tensor_tensor(out=picked[:, :, :], in0=picked[:, :, :], scalar=0.0,
                                                    in1=aff[:, :, :], op0=ALU.max, op1=ALU.subtract))
                link(nc.vector.tensor_reduce(rsum[:, 0, :], picked[:, :, :], AX.X, ALU.add))
                link(nc.vector.tensor_scalar(rsum[:, 1, :], rsum[:, 0, :], -1e-9, None, ALU.add))
                yield 16
                mask_rows(picked[:, :, :], E0, c)
                yield 17
                dve.wait_ge(pe_z, at(1))
                nc.vector.scalar_tensor_tensor(out=z_t, in0=u_t, scalar=vec[:, V_D:V_D + 1], in1=ps[:, B_BANK, :],
                                               op0=ALU.mult, op1=ALU.add).then_inc(z_done, 1)
                yield 20
                dve.wait_ge(pe_zt, at(1))
                link(nc.vector.tensor_tensor(x2, xn[:, :, :], bank_rows(A_BANK), ALU.add))
                yield from norm(x2, c["norm_done"], 21, 22, 23)
                yield 31
                dve.wait_ge(pe_z2t, at(1))
                nc.vector.tensor_tensor(s_rows[:, half, :, :], x2, bank_rows(B_BANK), ALU.add).then_inc(s_done, 1)

            def prelude1(b, half):
                c = L[1]

                def at(k, per=1):
                    return nth(b, half, per, k)

                yield 5
                dve.wait_ge(s_xln, 16 * at(1 + CHUNKS))
                yield from norm(x_ln, c["norm_done"], 5, 6, 7)
                yield 10
                dve.wait_ge(c["xhi_done"], at(1))
                nc.vector.tensor_tensor(x_lo[:, half, :], ps[:, A_BANK, :], x_hi[:, half, :].bitcast(F),
                                        ALU.subtract).then_inc(c["xlo_done"], 1)
                yield 15
                dve.wait_ge(c["pe_logits"], at(1))
                lg = aff[:, :, 0:E1]
                link(nc.vector.tensor_tensor(lg, ps[:, A_BANK, 0:NT * E1].rearrange("p (t e) -> p t e", t=NT),
                                             bias_sb[:, :].unsqueeze(1).to_broadcast([P, NT, E1]), ALU.add))
                link(nc.vector.tensor_reduce(rsum[:, 0, :], lg, AX.X, ALU.max))
                nc.vector.tensor_tensor(lg, lg, spread(rsum[:, 0, :], E1), ALU.subtract).then_inc(logit_done, 1)
                yield 16
                dve.wait_ge(score_exp, at(1))
                link(nc.vector.tensor_reduce(rsum[:, 0, :], lg, AX.X, ALU.add))
                link(nc.vector.reciprocal(rsum[:, 1, :], rsum[:, 0, :]))
                link_alone(nc.vector.tensor_tensor(scores1[:, :, 0:E1], lg, spread(rsum[:, 1, :], E1), ALU.mult))
                yield 17
                for t in range(NT):
                    last = nc.vector.max(top8[:, t, :], scores1[:, t, 0:E1])
                link(last)
                link_alone(nc.vector.memset(top8[:, :, 4:8], -1.0))
                yield 18
                for t in range(NT):
                    last = nc.vector.match_replace(aff[:, t, 0:E1 + 4], top8[:, t, :], scores1[:, t, :], -2.0)
                link(last)
                yield 19
                pk = picked[:, :, 0:E1]
                link(nc.vector.scalar_tensor_tensor(out=pk, in0=aff[:, :, 0:E1], scalar=0.0, in1=scores1[:, :, 0:E1],
                                                    op0=ALU.max, op1=ALU.subtract))
                link(nc.vector.tensor_reduce(rsum[:, 0, :], pk, AX.X, ALU.add))
                link(nc.vector.tensor_scalar(rsum[:, 1, :], rsum[:, 0, :], -1e-12, None, ALU.min))
                yield 20
                mask_rows(pk, E1, c)

            def splits(ahead):
                def split(t):
                    t += ahead
                    if not 0 <= t < U1:
                        return
                    dve.wait_ge(whi_done[1], t + 1)
                    r, _ = staged(1, t)
                    nc.vector.tensor_tensor(w_lo[:, t, :, :].rearrange("p a b -> p (a b)"), stage[:, r, :],
                                            w_hi[:, t, :, :].rearrange("p a b -> p (a b)").bitcast(F),
                                            ALU.subtract).then_inc(wlo_done[1], 1)
                return split

            def chunk(layer, b, half, beside, first=False, final=False, split=None):
                n, c, units, masked = N[layer], L[layer], UNITS[layer], MASKED[layer]

                def experts_out(k):
                    dve.wait_ge(y_tanh, nth(b, half, 1, k))
                    nc.vector.scalar_tensor_tensor(out=g_t[:, :], in0=g_t[:, :], scalar=1.0, in1=ps[:, Y_BANK, :],
                                                   op0=ALU.add, op1=ALU.mult).then_inc(c["y_done"], 1)

                def residual(k):
                    dve.wait_ge(c["pe_gt"], nth(b, half, 1, k))
                    dve.wait_ge(s_xres, 16 * nth(b, half, 1, k + layer * CHUNKS))
                    nc.vector.scalar_tensor_tensor(
                        out=rows[:, :, :].rearrange("p t d -> p (t d)"),
                        in0=s_rows[:, half if k else 1 - half, :, :].rearrange("p t d -> p (t d)"), scalar=0.5 if layer else 1.0,
                        in1=ps[:, A_BANK, :], op0=ALU.mult, op1=ALU.mult).then_inc(c["gated"], 1)

                def hidden(t):
                    a = slot(layer, half, t)
                    bank = 2 * pair_of(layer, half, "unit", t)
                    g, hd = gate[:, a, :], hid[:, a, :]
                    dve.wait_ge(n["gate_act"], nth(b, half, units, t + 1))
                    if layer:
                        nc.vector.scalar_tensor_tensor(out=g, in0=g, scalar=1.0, in1=ps[:, bank, :], op0=ALU.add,
                                                       op1=ALU.mult).then_inc(n["gate_done"], 1)
                        dve.wait_ge(n["gate_done"], nth(b, half, units, t + 1))
                    dve.wait_ge(n["pe_u"], nth(b, half, units, t + 1))
                    if t < masked:
                        nc.vector.tensor_tensor(g, g, ps[:, bank + 1, :], ALU.mult).then_inc(n["prod_done"], 1)
                        dve.wait_ge(n["prod_done"], nth(b, half, masked, t + 1))
                        dve.wait_ge(n["pe_m"], nth(b, half, masked, t + 1))
                    if not first or t >= 2:
                        dve.wait_ge(n["hlo_done"], nth(b, half, units, t - 1))
                    other = ps[:, M_BANK if t < masked else bank + 1, :]
                    if layer:
                        ins = nc.vector.scalar_tensor_tensor(out=hd, in0=g, scalar=0.5, in1=other, op0=ALU.mult, op1=ALU.mult)
                    else:
                        ins = nc.vector.tensor_tensor(hd, g, other, ALU.mult)
                    ins.then_inc(n["hid_done"], 1)

                for kind, t in ORDER[layer][half]:
                    if kind == "unit":
                        hidden(t)
                        if layer and t == 0:
                            dve.wait_ge(c["xn_done"], nth(b, half, 1, 1))
                            nc.vector.tensor_copy(values[:, half * NT:(half + 1) * NT, :, 0:HD],
                                                  xn[:, :, :].rearrange("p t (h c) -> p t h c", c=HD)).then_inc(val_done, 1)
                        if layer and not first and t == LAG - 1:
                            experts_out(0)
                        if not first and t == LAG + 1:
                            residual(0)
                        beside.after(t)
                        if split is not None:
                            split(t)
                    elif kind == "stack":
                        dve.wait_ge(pe_stack, nth(b, half, HG, t + 1))
                        nc.vector.tensor_copy(k_stack[:, t, half * CH:(half + 1) * CH],
                                              ps[:, 2 * pair_of(layer, half, kind, t) + 1, :]).then_inc(k_done, 1)
                    else:
                        if last_of_group(half, t - 1):
                            dve.wait_ge(pe_pv, b * ALL_STEPS + STEP0[half] + t)
                            nc.vector.tensor_copy(heads_out[:, :], ps[:, O_BANK, :]).then_inc(o_done, 1)
                        if last_of_group(half, t - 3):
                            g = STEPS[half][t - 3][0]
                            dve.wait_ge(pe_ot, nth(b, half, HG, g + 1))
                            o = ps[:, A_BANK, :].rearrange("p (t j c) -> p t j c", t=NT, j=4)
                            link(nc.vector.reciprocal(rden[:, :, :], o[:, :, :, HD]))
                            nc.vector.tensor_tensor(
                                s_rows[:, half, :, g * 32:(g + 1) * 32].rearrange("p t (j c) -> p t j c", j=4),
                                o[:, :, :, 0:HD], rden[:, :, :].unsqueeze(3).to_broadcast([P, NT, 4, HD]),
                                ALU.mult).then_inc(so_done, 1)
                if final:
                    if layer:
                        experts_out(1)
                    residual(1)
                beside.after(units)

            first_prelude = Beside(prelude0(0, 0))
            first_prelude.after(2)
            dve.wait_ge(s_small, 80)
            nc.vector.memset(scores1[:, :, E1:E1 + 4], -1.0)
            nc.vector.memset(values[:, :, :, HD:VW], 1.0)
            link(nc.vector.tensor_copy(router_hi[:, :], small_sb[:, S_R0:S_END]))
            nc.vector.tensor_tensor(router_lo[:, :], small_sb[:, S_R0:S_END], router_hi[:, :].bitcast(F),
                                    ALU.subtract).then_inc(setup_dve, 1)
            dve.wait_ge(setup_act, 1)
            link(nc.vector.tensor_scalar(lam[:, 1:2], lam[:, 0:1], 1.0, None, ALU.add))
            link(nc.vector.reciprocal(lam[:, 0:1], lam[:, 1:2]))
            nc.vector.tensor_scalar(lam[:, 2:3], lam[:, 0:1], -1.0, 1.0, ALU.mult, ALU.add).then_inc(setup_dve, 1)
            first_prelude.after(8)
            nc.vector.tensor_copy(sel0[:, :].rearrange("p (e i) -> p e i", e=E0),
                                  cst[:, C_OH0:C_OH0 + E0].unsqueeze(2).to_broadcast([P, E0, I0])).then_inc(setup_dve, 1)
            first_prelude.after(FIRST_PART)

            def inner(layer, per_sequence, pre):
                before = state["n"]
                with dve.Fori(0, SEQS - 1) as b:
                    state.update(n=before, b=b * per_sequence)
                    chunk(layer, b, 1, Beside(pre(b + 1, 0)))
                    chunk(layer, b + 1, 0, Beside(pre(b + 1, 1)))
                if state["n"] - before != per_sequence:
                    raise ValueError(f"layer {layer}: {state['n'] - before} steps a sequence")
                state.update(n=before + (SEQS - 1) * per_sequence, b=0)

            chunk(0, 0, 0, CatchUp(first_prelude, Beside(prelude0(0, 1))), first=True)
            inner(0, V0_STEPS, prelude0)
            chunk(0, SEQS - 1, 1, Beside(prelude1(0, 0)), final=True, split=splits(-9))
            chunk(1, 0, 0, Beside(prelude1(0, 1)), first=True, split=splits(U0 - 9))
            inner(1, V1_STEPS, prelude1)
            chunk(1, SEQS - 1, 1, Beside(), final=True)

        @block.gpsimd
        def _(pool):
            def chunk(layer, b, half, first=False, final=False):
                n, units = N[layer], UNITS[layer]

                def lo(t):
                    a, to = slot(layer, half, t), part_slot(layer, half, t)
                    pool.wait_ge(n["hhi_done"], nth(b, half, units, t + 1))
                    if not first or t >= LAG:
                        pool.wait_ge(n["pe_down"], nth(b, half, units, t + 1 - LAG))
                    nc.gpsimd.tensor_tensor(h_lo[:, to, :], hid[:, a, :], h_hi[:, to, :].bitcast(F),
                                            ALU.subtract).then_inc(n["hlo_done"], 1)

                def residual(k):
                    pool.wait_ge(L[layer]["gated"], nth(b, half, 1, k))
                    nc.gpsimd.tensor_tensor(x_res[:, :, :], x_res[:, :, :], rows[:, :, :],
                                            ALU.add).then_inc(L[layer]["x_new"], 1)

                for kind, t in ORDER[layer][half]:
                    if kind == "unit":
                        if not first or t >= 1:
                            lo(t - 1)
                        if not first and t == LAG + 2:
                            residual(0)
                        if layer == 0 and first and t + AHEAD < U0:
                            split_lo(t + AHEAD)
                    elif kind == "step" and t < len(STEPS[half]) and diagonal(half, STEPS[half][t][1]):
                        step, c0 = STEP0[half] + t, first_col(half, STEPS[half][t][1])
                        for p in range(2):
                            pool.wait_ge(exp_done, b * (2 * ALL_STEPS) + 2 * step + p + 1)
                            pool.sem_inc(waited_pool, 1)
                            part = prob[:, step % 2, 2 * p:2 * p + 2, c0:c0 + P]
                            nc.gpsimd.affine_select(out=part, in_=part, compare_op=ALU.is_ge, fill=0.0, base=0,
                                                    pattern=[[0, 2], [1, P]], channel_multiplier=-1)\
                                .then_inc(causal_done, 1)
                if final:
                    lo(units - 1)
                    residual(1)

            def split_lo(t):
                pool.wait_ge(whi_done[0], t + 1)
                nc.gpsimd.tensor_tensor(w_lo[:, t, :, :].rearrange("p a b -> p (a b)"), stage[:, t % RING, :],
                                        w_hi[:, t, :, :].rearrange("p a b -> p (a b)").bitcast(F),
                                        ALU.subtract).then_inc(wlo_done[0], 1)

            for t in range(AHEAD):
                split_lo(t)
            for layer in range(2):
                chunk(layer, 0, 0, first=True)
                with pool.Fori(0, SEQS - 1) as b:
                    chunk(layer, b, 1)
                    chunk(layer, b + 1, 0)
                chunk(layer, SEQS - 1, 1, final=True)

        @block.tensor
        def _(pe):
            mm = nc.tensor.matmul

            def transposes(bank, src, done):
                for t in range(NT):
                    last = nc.tensor.transpose(ps[:, bank, t * P:(t + 1) * P], src(t), ident)
                last.then_inc(done, 1)

            def split3(dst, w0, w1, m0, m1, start, stop):
                mm(dst, w0, m0, start=start, stop=False)
                mm(dst, w0, m1, start=False, stop=False)
                return mm(dst, w1, m0, start=False, stop=stop)

            def logits(experts, c0, half):
                for t in range(NT):
                    dst = ps[:, A_BANK, t * experts:(t + 1) * experts]
                    xs = [a[:, half, t * P:(t + 1) * P] for a in (x_hi, x_lo)]
                    ws = [a[:, c0:c0 + experts] for a in (router_hi, router_lo)]
                    terms = [(x_, w_) for x_ in xs for w_ in ws]
                    for i, (x_, w_) in enumerate(terms):
                        last = mm(dst, x_, w_, start=i == 0, stop=i == 3)
                return last

            a_read = []

            def use_a(reader):
                for waited in a_read:
                    pe.wait_ge(*waited)
                a_read[:] = [reader]

            def prelude0(b, half):
                c = L[0]

                def at(k, per=1):
                    return nth(b, half, per, k)

                yield 6
                pe.wait_ge(c["xn_done"], at(1))
                gated = nth(b, half, 1, -1)
                if not isinstance(gated, int) or gated > 0:
                    pe.wait_ge(c["gated"], gated)
                transposes(A_BANK, lambda t: xn[:, t, :], c["pe_xt"])
                yield 9
                pe.wait_ge(c["xlo_done"], at(1))
                logits(E0, 0, half).then_inc(c["pe_logits"], 1)
                yield 10
                pe.wait_ge(u0_done, at(1))
                transposes(B_BANK, lambda t: rows[:, t, :], pe_ut)
                yield 12
                pe.wait_ge(aff_exp, at(1))
                pe.wait_ge(u_done, at(1))
                mm(ps[:, A_BANK, :], small_sb[:, S_IN:S_IN + P], u_t, start=True, stop=True).then_inc(pe_up, 1)
                yield 16
                pe.wait_ge(y_scan, at(1))
                mm(ps[:, B_BANK, :], small_sb[:, S_OUT:S_OUT + P], y_t, start=True, stop=True).then_inc(pe_z, 1)
                yield 18
                pe.wait_ge(c["mask_rows"], at(1))
                transposes(A_BANK, lambda t: msk[:, t, :], c["pe_mask"])
                yield 20
                pe.wait_ge(c["mask_done"], at(1))
                pe.wait_ge(z_done, at(1))
                transposes(A_BANK, lambda t: z_t[:, t * P:(t + 1) * P], pe_zt)
                yield 25
                pe.wait_ge(h0_done, at(1))
                transposes(B_BANK, lambda t: rows[:, t, :], pe_ht)
                yield 27
                pe.wait_ge(h_done, at(1))
                for i, bank in enumerate((A_BANK, B_BANK)):
                    mm(ps[:, bank, :], small_sb[:, S_W1 + i * P:S_W1 + (i + 1) * P], v_t,
                       start=True, stop=True).then_inc(pe_f, 1)
                yield 29
                pe.wait_ge(relu_done, at(2, 2))
                for i in range(2):
                    last = mm(ps[:, A_BANK, :], small_sb[:, S_W2 + i * P:S_W2 + (i + 1) * P], relu[:, i, :],
                              start=i == 0, stop=i == 1)
                last.then_inc(pe_z2, 1)
                yield 31
                pe.wait_ge(z2_done, at(1))
                transposes(B_BANK, lambda t: z_t[:, t * P:(t + 1) * P], pe_z2t)

            def prelude1(b, half):
                c = L[1]

                def at(k, per=1):
                    return nth(b, half, per, k)

                yield 9
                pe.wait_ge(c["xn_done"], at(1))
                use_a((c["xlo_done"], at(1)))
                transposes(A_BANK, lambda t: xn[:, t, :], c["pe_xt"])
                yield 15
                use_a((logit_done, at(1)))
                logits(E1, E0, half).then_inc(c["pe_logits"], 1)
                yield 22
                pe.wait_ge(c["mask_rows"], at(1))
                use_a((c["mask_done"], at(1)))
                transposes(A_BANK, lambda t: msk[:, t, :], c["pe_mask"])

            def pair_readers(layer, b, half):
                n = N[layer]
                for kind, t in ORDER[layer][half]:
                    if kind == "unit":
                        yield ((n["prod_done"], nth(b, half, MASKED[layer], t + 1)) if t < MASKED[layer] else
                               (n["hid_done"], nth(b, half, UNITS[layer], t + 1)),)
                    elif kind == "stack":
                        yield (q_done, nth(b, half, HG, t + 1)), (k_done, nth(b, half, HG, t + 1))
                    elif t < len(STEPS[half]):
                        for p in range(2):
                            yield ((exp_done, b * (2 * ALL_STEPS) + 2 * (STEP0[half] + t) + p + 1),)

            def chunk(layer, b, half, beside, first=False, final=False):
                n, c, units, masked = N[layer], L[layer], UNITS[layer], MASKED[layer]
                before = [()] * 2 if first else list(pair_readers(layer, *((b, 0) if half else (b - 1, 1))))[-2:]
                readers = iter(before + list(pair_readers(layer, b, half)))

                def pair(kind, t, p=0):
                    for waited in next(readers):
                        pe.wait_ge(*waited)
                    return 2 * pair_of(layer, half, kind, t, p)

                def down(t):
                    a, w = part_slot(layer, half, t), t % units
                    pe.wait_ge(n["hlo_done"], nth(b, half, units, t + 1))
                    split3(ps[:, Y_BANK, :], w_hi[:, w, 2, :], w_lo[:, w, 2, :], h_hi[:, a, :], h_lo[:, a, :],
                           w == 0, w == units - 1).then_inc(n["pe_down"], 1)

                def gate_rows(k):
                    if layer:
                        pe.wait_ge(so_done, nth(b, half, HG, k * HG))
                        a_read[:] = [(c["gated"], nth(b, half, 1, k))]
                    pe.wait_ge(c["y_done"], nth(b, half, 1, k))
                    transposes(A_BANK, lambda t: g_t[:, t * P:(t + 1) * P], c["pe_gt"])

                def values_product(s):
                    g, k = STEPS[half][s]
                    step, c0 = STEP0[half] + s, first_col(half, k)
                    if s == 0:
                        pe.wait_ge(val_done, nth(b, half, 1, 1))
                    pe.wait_ge(exp_done, b * (2 * ALL_STEPS) + 2 * step + 2)
                    if diagonal(half, k):
                        pe.wait_ge(causal_done, b * ALL_CAUSAL + causal_after(half, s))
                    if k == 0 and g > 0:
                        pe.wait_ge(o_done, nth(b, half, HG, g))
                    for j in range(4):
                        last = mm(ps[32 * j:32 * j + VW, O_BANK, c0:CH], values[:, k, 4 * g + j, :],
                                  prob[:, step % 2, j, c0:CH], start=k == 0, stop=k == NT * (half + 1) - 1)
                    last.then_inc(pe_pv, 1)

                def rest_of_unit(t):
                    if t == LAG and not first:
                        pe.wait_ge(c["y_done"], nth(b, half, 1, 0))
                    if t >= LAG or not first:
                        down(t - LAG)
                    if t < masked:
                        if t == 0:
                            pe.wait_ge(c["mask_done"], nth(b, half, 1, 1))
                        if not first or t >= 1:
                            pe.wait_ge(n["hid_done"], nth(b, half, units, t))
                        if layer == 0:
                            last = mm(ps[:, M_BANK, :], sel0[:, t * P:(t + 1) * P], mask_t[:, half, :], start=True, stop=True)
                        else:
                            last = mm(ps[:, M_BANK, :], onehot1[:, t:t + 1].to_broadcast([2 * E1, P]),
                                      mask_t[0:2 * E1, half, :], start=True, stop=True)
                        last.then_inc(n["pe_m"], 1)
                    if t == LAG and not first:
                        gate_rows(0)
                    beside.after(t)

                xh, xl = x_hi[:, half, :], x_lo[:, half, :]
                rest = None
                for kind, t in ORDER[layer][half]:
                    if rest is not None and (kind != "step" or t >= len(STEPS[half])):
                        rest_of_unit(rest)
                        rest = None
                    if kind == "unit":
                        if first:
                            pe.wait_ge(wlo_done[layer], t + 1)
                        bank = pair(kind, t)
                        split3(ps[:, bank, :], w_hi[:, t, 0, :], w_lo[:, t, 0, :], xh, xl, True, True).then_inc(n["pe_g"], 1)
                        split3(ps[:, bank + 1, :], w_hi[:, t, 1, :], w_lo[:, t, 1, :], xh, xl, True, True).then_inc(n["pe_u"], 1)
                        rest = t
                    elif kind == "stack":
                        bank = pair(kind, t)
                        r = slice(32 * t, 32 * t + 32)
                        for which in range(2):
                            mm(ps[:, bank + which, :], sel[r, 2 * which, :], xh[r, :], start=True, stop=False)
                            last = mm(ps[:, bank + which, :], sel[r, 2 * which + 1, :], xl[r, :], start=False, stop=True)
                        last.then_inc(pe_stack, 1)
                    else:
                        if t < len(STEPS[half]):
                            g, k = STEPS[half][t]
                            step, c0 = STEP0[half] + t, first_col(half, k)
                            if k == 0:
                                pe.wait_ge(q_done, nth(b, half, HG, g + 1))
                                pe.wait_ge(k_done, nth(b, half, HG, g + 1))
                            for p in range(2):
                                if p == 1:
                                    if rest is not None:
                                        rest_of_unit(rest)
                                        rest = None
                                    if t >= 1:
                                        values_product(t - 1)
                                bank = pair(kind, t, p)
                                for j in (2 * p, 2 * p + 1):
                                    r = slice(32 * j, 32 * j + 32)
                                    last = mm(ps[:, bank + j % 2, c0:CH], k_stack[r, g, k * P:(k + 1) * P],
                                              q_stack[r, g, c0:CH], start=True, stop=True)
                                last.then_inc(pe_s, 1)
                        if t == len(STEPS[half]):
                            values_product(t - 1)
                        if last_of_group(half, t - 2):
                            g = STEPS[half][t - 2][0]
                            pe.wait_ge(o_done, nth(b, half, HG, g + 1))
                            use_a((so_done, nth(b, half, HG, g + 1)))
                            transposes(A_BANK, lambda t: heads_out[:, t * P:(t + 1) * P], pe_ot)
                if rest is not None:
                    rest_of_unit(rest)
                if final:
                    for t in range(units - LAG, units):
                        down(t)
                    gate_rows(1)
                beside.after(units)

            pe.wait_ge(s_small, 80)
            pe.wait_ge(setup_dve, 2)
            first_prelude = Beside(prelude0(0, 0))
            first_prelude.after(FIRST_PART)
            pe.wait_ge(setup_dve, 3)
            chunk(0, 0, 0, CatchUp(first_prelude, Beside(prelude0(0, 1))), first=True)
            with pe.Fori(0, SEQS - 1) as b:
                chunk(0, b, 1, Beside(prelude0(b + 1, 0)))
                chunk(0, b + 1, 0, Beside(prelude0(b + 1, 1)))
            a_read[:] = [(L[0]["gated"], CHUNKS - 1)]
            chunk(0, SEQS - 1, 1, Beside(prelude1(0, 0)), final=True)
            pe.wait_ge(setup_act, 3)
            a_read.clear()
            chunk(1, 0, 0, Beside(prelude1(0, 1)), first=True)
            with pe.Fori(0, SEQS - 1) as b:
                chunk(1, b, 1, Beside(prelude1(b + 1, 0)))
                chunk(1, b + 1, 0, Beside(prelude1(b + 1, 1)))
            chunk(1, SEQS - 1, 1, Beside(), final=True)


def _pairs():
    table = {}
    for layer, orders in enumerate(((ORDER0, ORDER0), ORDER1)):
        i = 0
        for half, order in enumerate(orders):
            for kind, t in order:
                uses = 0 if kind == "step" and t >= len(STEPS[half]) else 2 if kind == "step" else 1
                for p in range(uses):
                    table[layer, half, kind, t, p] = i % 2
                    i += 1
        assert i % 2 == 0
    return table


PAIRS = _pairs()


def pair_of(layer, half, kind, t, p=0):
    return PAIRS[layer, half, kind, t, p]


def _units(parts, units):
    import numpy as np
    w = np.zeros((units, P, 3, P), np.float32)
    for at, n, gate_, up_, down_ in parts:
        w[at:at + n, :, 0, :gate_.shape[2]] = gate_
        w[at:at + n, :, 1, :up_.shape[2]] = up_
        w[at:at + n, :down_.shape[1], 2, :] = down_
    return w.reshape(units, P, 3 * P)


def _constants():
    import numpy as np
    c = np.zeros((P, C_END), np.float32)
    k = np.arange(P)
    c[k, C_ID + k] = 1.0
    c[k, C_OH0 + k % E0] = 1.0
    c[k, C_OH1 + k % E1] = 1.0
    for n, slots in enumerate(((0, 1), (2, 3), (0, 2), (1, 3))):
        for a in slots:
            r = k % 32
            c[k, C_SEL + n * P + 32 * (r // 8) + 8 * a + r % 8] = 1.0
    return c


def kernel(**inputs):
    import numpy as np
    import concourse.bacc as bacc
    from concourse.bass_utils import run_bass_kernel_spmd

    a = {k: np.asarray(v) for k, v in inputs.items()}

    def pairs(w):
        return w.reshape(M0, 2, P, I0).transpose(0, 2, 1, 3).reshape(M0, P, P)

    w0 = _units([
        (0, M0, pairs(a["L0_ffn_expert_gate_k"]), pairs(a["L0_ffn_expert_up_k"]), a["L0_ffn_expert_down_k"].reshape(M0, P, D)),
        (M0, 1, a["L0_ffn_shared_gate_w"][None], a["L0_ffn_shared_up_w"][None], a["L0_ffn_shared_down_w"][None]),
    ], U0)
    S = U1 - M1
    w1 = _units([
        (0, M1, *(a[f"L1_ffn_{n}_w"].transpose(0, 2, 1) for n in ("gate", "up", "down"))),
        (M1, S, *(a[f"L1_ffn_{n}_w"].reshape(S, P, D).transpose(0, 2, 1) for n in ("sgate", "sup")),
         a["L1_ffn_sdown_w"].T.reshape(S, P, D)),
    ], U1)
    small = np.concatenate([
        a["L0_attn_w_in"].T, a["L0_attn_w_out"].T, a["L0_attn_w1"].T,
        a["L0_attn_w2"].T.reshape(2, P, D).transpose(1, 0, 2).reshape(P, 2 * D),
        a["L0_ffn_router_w"], a["L1_ffn_router_w"].T], axis=1)
    vectors = np.stack([a["L0_attn_log_lambda"], a["L0_attn_D_skip"], a["L0_attn_ln1_g"], a["L0_attn_ln1_b"],
                        a["L0_attn_ln2_g"], a["L0_attn_ln2_b"], a["L0_attn_b1"][:P], a["L0_attn_b1"][P:],
                        a["L0_attn_b2"]], axis=1)
    arrays = {
        "x_dram": a["L0_attn_x"].reshape(SEQS * T, D), "weights0_dram": w0, "weights1_dram": w1,
        "small_dram": small, "vectors_dram": vectors, "bias1_dram": a["L1_ffn_router_bias"],
        "constants_dram": _constants(),
    }
    arrays = {k: np.ascontiguousarray(v) for k, v in arrays.items()}
    nc = bacc.Bacc("TRN2", target_bir_lowering=False, num_devices=1, dynamic_dma_scratch_size=1024)
    args = [nc.dram_tensor(k, v.shape, mybir.dt.from_np(v.dtype), kind="ExternalInput").ap() for k, v in arrays.items()]
    out = nc.dram_tensor("out_dram", (SEQS * T, D), mybir.dt.float32, kind="ExternalOutput").ap()
    x1 = nc.dram_tensor("x1_dram", (SEQS * T, D), mybir.dt.float32, kind="Internal").ap()
    two_layers(nc, *args, x1, out)
    r = run_bass_kernel_spmd(nc, [arrays], core_ids=[0])
    return r.results[0]["out_dram"].reshape(SEQS, T, D)
```
